# Optimizing a Trainium2 kernel written in Bass

```python
import numpy as np
import jax
import jax.numpy as jnp

def _softmax(x, axis=-1):
    return jax.nn.softmax(x, axis=axis)

def _gelu(x):
    return jax.nn.gelu(x, approximate=True)

def _silu(x):
    return jax.nn.silu(x)

def _sigmoid(x):
    return jax.nn.sigmoid(x)

def _layernorm(x, axis=-1, eps=1e-05):
    m = jnp.mean(x, axis=axis, keepdims=True)
    v = jnp.var(x, axis=axis, keepdims=True)
    return (x - m) / jnp.sqrt(v + eps)

def _scatter_add(tgt, idx, src, axis=0):
    return tgt.at[idx].add(src)

def _segment_sum(src, seg, n):
    return jax.ops.segment_sum(src, seg, n)
kernel_name = 'mk_gnn_preln_d2_gnn_r32_da268c'

def setup_inputs(seed: int=0):
    np.random.seed(seed)
    _w = jnp.asarray

    def _rec_inputs():
        import jax
        import jax.numpy as jnp
        _gk = jax.random.key(seed)
        x = -0.000202 + 1 * jax.random.normal(jax.random.fold_in(_gk, 1), (3125, 128), jnp.float32)
        _s = jax.random.randint(jax.random.fold_in(_gk, 2), (25000,), 0, 3125, jnp.int32)
        _d = jax.random.randint(jax.random.fold_in(_gk, 3), (25000,), 0, 3125, jnp.int32)
        _loop = jnp.arange(3125, dtype=jnp.int32)
        src = jnp.concatenate([_s, _d, _loop])
        dst = jnp.concatenate([_d, _s, _loop])
        _o = jnp.argsort(dst, stable=True)
        src = src[_o]
        dst = dst[_o]
        edge_attr_128 = -5.16925e-05 + 1.00005 * jax.random.normal(jax.random.fold_in(_gk, 13), (53125, 128), jnp.float32)
        return (x, src, dst, edge_attr_128)
    x, src, dst, edge_attr_128 = _rec_inputs()

    def _L0_gnn_setup():
        import jax
        import jax.numpy as jnp
        import numpy as np
        N_NODES = 50000
        N_EDGES = 50000
        D_IN = 128
        D_EDGE = 64
        D_NODE = 128
        key = jax.random.key(seed)
        ks = jax.random.split(key, 9)
        s = 0.05
        return {'node_features': jax.random.normal(ks[0], (N_NODES, D_IN), dtype=jnp.float32), 'W_fs': jax.random.normal(ks[1], (D_IN, D_EDGE), dtype=jnp.float32) * s, 'b_fs': jax.random.normal(ks[2], (D_EDGE,), dtype=jnp.float32) * s, 'W_gn': jax.random.normal(ks[3], (D_IN, D_NODE), dtype=jnp.float32) * s, 'b_gn': jax.random.normal(ks[4], (D_NODE,), dtype=jnp.float32) * s, 'W_gin': jax.random.normal(ks[5], (D_EDGE, D_NODE), dtype=jnp.float32) * s, 'b_gin': jax.random.normal(ks[6], (D_NODE,), dtype=jnp.float32) * s, 'senders': jax.random.randint(ks[7], (N_EDGES,), 0, N_NODES, dtype=jnp.int32), 'receivers': jax.random.randint(ks[8], (N_EDGES,), 0, N_NODES, dtype=jnp.int32)}
    _L0_gnn_all = _L0_gnn_setup()
    _L0_gnn_in = {k: v for k, v in _L0_gnn_all.items() if k in ('W_fs', 'b_fs', 'W_gn', 'b_gn', 'W_gin', 'b_gin')}
    del _L0_gnn_all

    def _L1_gnn_setup():
        import jax, jax.numpy as jnp
        import numpy as np
        N, E, B = (50000, 25000, 16)
        DX = DE = DU = DO = 128
        IN1 = 2 * DX + DE + DU
        IN2 = DX + DO + DU
        key = jax.random.key(seed)
        ks = jax.random.split(key, 9)
        x = jax.random.normal(ks[0], (N, DX), dtype=jnp.float32)
        edge_index = jax.random.randint(ks[1], (2, E), 0, N, dtype=jnp.int64)
        edge_attr = jax.random.normal(ks[2], (E, DE), dtype=jnp.float32)
        u = jax.random.normal(ks[3], (B, DU), dtype=jnp.float32)
        batch = jnp.sort(jax.random.randint(ks[4], (N,), 0, B, dtype=jnp.int64))
        W1 = jax.random.normal(ks[5], (DO, IN1), dtype=jnp.float32) / np.sqrt(IN1)
        b1 = jnp.zeros((DO,), dtype=jnp.float32)
        W2 = jax.random.normal(ks[6], (DO, IN2), dtype=jnp.float32) / np.sqrt(IN2)
        b2 = jnp.zeros((DO,), dtype=jnp.float32)
        return {'x': x, 'edge_index': edge_index, 'edge_attr': edge_attr, 'u': u, 'batch': batch, 'W1': W1, 'b1': b1, 'W2': W2, 'b2': b2}
    _L1_gnn_all = _L1_gnn_setup()
    _L1_gnn_in = {k: v for k, v in _L1_gnn_all.items() if k in ('u', 'W1', 'b1', 'W2', 'b2')}
    del _L1_gnn_all
    return {'x': x, 'src': src, 'dst': dst, 'edge_attr_128': edge_attr_128, 'L0_gnn_W_fs': _L0_gnn_in['W_fs'], 'L0_gnn_b_fs': _L0_gnn_in['b_fs'], 'L0_gnn_W_gn': _L0_gnn_in['W_gn'], 'L0_gnn_b_gn': _L0_gnn_in['b_gn'], 'L0_gnn_W_gin': _L0_gnn_in['W_gin'], 'L0_gnn_b_gin': _L0_gnn_in['b_gin'], 'L1_gnn_u': _L1_gnn_in['u'], 'L1_gnn_W1': _L1_gnn_in['W1'], 'L1_gnn_b1': _L1_gnn_in['b1'], 'L1_gnn_W2': _L1_gnn_in['W2'], 'L1_gnn_b2': _L1_gnn_in['b2']}

def reference(x, src, dst, edge_attr_128, L0_gnn_W_fs, L0_gnn_b_fs, L0_gnn_W_gn, L0_gnn_b_gn, L0_gnn_W_gin, L0_gnn_b_gin, L1_gnn_u, L1_gnn_W1, L1_gnn_b1, L1_gnn_W2, L1_gnn_b2):
    import jax
    import jax.numpy as jnp

    def _L0_gnn_ref(node_features, W_fs, b_fs, W_gn, b_gn, W_gin, b_gin, senders, receivers):
        import jax
        import jax.numpy as jnp
        import numpy as np
        N_NODES = 50000
        N_EDGES = 50000
        D_IN = 128
        D_EDGE = 64
        D_NODE = 128
        num_nodes = node_features.shape[0]
        proj = node_features @ W_fs + b_fs
        edges = jax.nn.relu(proj[senders])
        agg = jax.ops.segment_max(edges, receivers, num_segments=num_nodes)
        agg = jnp.where(jnp.isfinite(agg), agg, jnp.zeros((), dtype=agg.dtype))
        nodes = node_features @ W_gn + b_gn + (agg @ W_gin + b_gin)
        return nodes

    def _L1_gnn_ref(x, edge_index, edge_attr, u, batch, W1, b1, W2, b2):
        import jax, jax.numpy as jnp
        import numpy as np
        N, E, B = (50000, 25000, 16)
        DX = DE = DU = DO = 128
        IN1 = 2 * DX + DE + DU
        IN2 = DX + DO + DU
        col, row = (edge_index[0], edge_index[1])
        msg_in = jnp.concatenate([x[row], x[col], edge_attr, u[batch[row]]], axis=1)
        edge_messages = jax.nn.relu(msg_in @ W1.T + b1)
        aggregated = jax.ops.segment_sum(edge_messages, row, num_segments=x.shape[0])
        node_in = jnp.concatenate([x, aggregated, u[batch]], axis=1)
        return jax.nn.relu(node_in @ W2.T + b2)
    edge_index = jnp.stack([src, dst])
    batch0 = jnp.zeros((3125,), jnp.int32)
    h = jnp.maximum(_layernorm(x, axis=-1), 0.0)
    x = x + _L0_gnn_ref(h, L0_gnn_W_fs, L0_gnn_b_fs, L0_gnn_W_gn, L0_gnn_b_gn, L0_gnn_W_gin, L0_gnn_b_gin, src, dst)
    h = jnp.maximum(_layernorm(x, axis=-1), 0.0)
    x = x + _L1_gnn_ref(h, edge_index, edge_attr_128, L1_gnn_u, batch0, L1_gnn_W1, L1_gnn_b1, L1_gnn_W2, L1_gnn_b2)
    return x

_drawn_inputs = setup_inputs


def setup_inputs(seed=0):
    import zlib

    import numpy as np

    out = dict(_drawn_inputs(seed))
    spreads = {'L1_gnn_b1': (0.0, 0.1), 'L1_gnn_b2': (0.0, 0.391)}
    factors = {'L0_gnn_b_fs': 6.759}
    for name, (base, spread) in spreads.items():
        noise = np.random.default_rng([zlib.crc32(name.encode()), seed]).standard_normal(out[name].shape)
        drawn = base * np.exp(spread * noise) if base else spread * noise
        out[name] = jnp.asarray(drawn.astype(out[name].dtype))
    for name, factor in factors.items():
        out[name] = (out[name] * factor).astype(out[name].dtype)
    return out
```

```python
import concourse.bass as bass
from concourse import mybir
from contextlib import ExitStack

N_NODES, N_EDGES, F, FE = 3125, 53125, 128, 64
P = 128
NT = -(-N_NODES // P)
NPAD = NT * P
TG = 5
NG = NT // TG
CH = 512
TPC = CH // P
RING = 4
NCH = -(-N_EDGES // (CH * 2 * RING)) * 2 * RING
EPAD = NCH * CH
HALF = EPAD // 2
NCH1 = NCH // 2
EC = EPAD // P
HC = EC // NCH1
EPS = 1e-5
DST_PAD = NPAD
SKIP = 1 << 17


def gnn_program(nc, x, src1, src2, dst, edge_t, w_fs, b_fs, w_gn, b_gn, w_gin, b_gin, u, w1_t, b1,
                w2_t, b2, out):
    fp32, bf16, i32, u8 = mybir.dt.float32, mybir.dt.bfloat16, mybir.dt.int32, mybir.dt.uint8
    ALU = mybir.AluOpType
    ACT = mybir.ActivationFunctionType

    with ExitStack() as ctx:
        def sb(name, shape, dt=fp32):
            return ctx.enter_context(nc.sbuf_tensor(name, shape, dt))

        def sem(name):
            return ctx.enter_context(nc.semaphore(name))

        def sems(name, n):
            return [sem(f"{name}{i}") for i in range(n)]

        p_tab = nc.dram_tensor("p_tab", (NPAD, FE), fp32).ap()
        b_tab = nc.dram_tensor("b_tab", (NPAD, F), fp32).ap()
        same_dram = nc.dram_tensor("same_dram", (1, EPAD), u8).ap()
        max_rows = nc.dram_tensor("max_rows", (HALF, 2 * FE), fp32).ap()
        seed_rows = nc.dram_tensor("seed_rows", (EPAD, F), fp32).ap()
        sum_rows = nc.dram_tensor("sum_rows", (EPAD, F), fp32).ap()

        ident = sb("ident", [P, P])
        below = sb("below", [P, P])
        iota_i = sb("iota_i", [P, P], i32)
        iota_bf = sb("iota_bf", [P, P], bf16)
        node_i = sb("node_i", [P, NT], i32)
        node_f = sb("node_f", [P, NT])
        zeros_bf = sb("zeros_bf", [P, P], bf16)
        zeros = sb("zeros", [P, 2 * TPC * F])
        ones = sb("ones", [1, P])
        eps = sb("eps", [P, 1])
        w0 = sb("w0", [P, FE + F])
        wgin = sb("wgin", [FE, F])
        w1 = sb("w1", [P, 4, F])
        w2 = sb("w2", [P, 3, F])
        w_aby = sb("w_aby", [P, 3 * F])
        u0 = sb("u0", [P, 1])
        bias_in = sb("bias_in", [1, 2 * F])
        bias0 = sb("bias0", [1, FE + F])
        b12 = sb("b12", [1, 2 * F])
        bias_aby = sb("bias_aby", [1, 3 * F])

        xs = sb("xs", [P, NT, F])
        ys = sb("ys", [P, NT, F])
        stats = sb("stats", [P, NT, 6])
        mv = sb("mv", [P, NT, 2])
        std = sb("std", [P, NT])
        rstd = sb("rstd", [P, NT])
        shift = sb("shift", [P, NT])
        h = sb("h", [P, 2, TG, F])
        ht = sb("ht", [P, 2, TG, F])
        p_out = sb("p_out", [P, 2, TG, FE])
        agg1 = sb("agg1", [P, NT, FE])
        carry = sb("carry", [P, FE])
        carried = sb("carried", [P, NT, FE])
        agg1_t = sb("agg1_t", [FE, 2, TG, P])
        place = sb("place", [P, HALF], u8)
        same1 = place[:, :]
        ab = place[:, 0:4 * NT * 2 * F].bitcast(fp32).rearrange("p (t c) -> p t c", t=NT)
        agg2 = ab

        dst_hi = sb("dst_hi", [P, EC], bf16)
        dst_lo = sb("dst_lo", [P, EC], bf16)
        same_row = sb("same_row", [P, EC], u8)
        same2 = sb("same2", [P, EPAD], u8)
        hot_lo = sb("hot_lo", [P, 2, HC, P], bf16)
        hot_hi = sb("hot_hi", [P, 2, HC, NT], bf16)
        count = sb("count", [NT, P])
        upto = sb("upto", [NT, P])
        end_row = sb("end_row", [NT, P])
        before = sb("before", [NT, 1])
        seg_end = sb("seg_end", [P, NT])
        seg_count = sb("seg_count", [P, NT])
        empty = sb("empty", [P, NT])
        filled = sb("filled", [P, NT])
        last_f = sb("last_f", [P, NT])
        upper = sb("upper", [P, NT])
        max_at_f = sb("max_at_f", [P, NT])
        seed_at_f = sb("seed_at_f", [P, NT])
        last_at = sb("last_at", [P, NT], i32)
        max_at = sb("max_at", [P, NT], i32)
        seed_at = sb("seed_at", [P, NT], i32)
        mid_i = sb("mid_i", [P, 1], i32)
        mid_f = sb("mid_f", [P, 1])
        is_mid = sb("is_mid", [P, NT])

        pick = sb("pick", [P, RING, 2 * TPC], i32)
        rows = sb("rows", [P, RING, TPC, F])
        edges = sb("edges", [P, RING, CH])
        dst_now, dst_before, dst_hi_i, dst_lo_i = (edges[:, k, 0:EC].bitcast(i32) for k in range(RING))
        seeds = sb("seeds", [P, RING, TPC, F])
        fill = sb("fill", [P, 2, CH])
        msg = sb("msg", [P, 2, CH])
        scan = sb("scan", [P, 2, CH])
        back = sb("back", [P, RING, CH])

        ps = [ctx.enter_context(nc.psum_tensor(f"ps{i}", [P, 2 * CH], fp32)) for i in range(4)]
        bank = [ps[i // 2][:, (i % 2) * CH:(i % 2 + 1) * CH] for i in range(8)]
        hist = bank[4][0:NT, 0:P]
        seg_ps = bank[4][:, P:P + 2 * NT]
        before_ps = bank[4][0:NT, 2 * P:2 * P + 1]
        bias_ps = bank[5][0:1, 0:2 * F]

        x_loaded = sems("x_loaded", NG)
        w0_loaded = sem("w0_loaded")
        w12_loaded = sem("w12_loaded")
        dst_loaded = sem("dst_loaded")
        mid_loaded = sem("mid_loaded")
        s_pool = sem("s_pool")
        consts = sem("consts")
        dve_consts = sem("dve_consts")
        iota_ready = sem("iota_ready")
        w_aby_ready = sem("w_aby_ready")
        bias0_ready = sem("bias0_ready")
        bias_made = sem("bias_made")
        bias_aby_ready = sem("bias_aby_ready")
        split_dst = sem("split_dst")
        same_made = sem("same_made")
        same_stored = sem("same_stored")
        same1_loaded = sem("same1_loaded")
        same2_loaded = sem("same2_loaded")
        stats_done = sem("stats_done")
        var_done = sem("var_done")
        std_done = sem("std_done")
        rstd_done = sem("rstd_done")
        norm_ready = sem("norm_ready")
        h_ready = sem("h_ready")
        ht_made = sem("ht_made")
        ht_ready = sem("ht_ready")
        prod0 = sem("prod0")
        p_taken = sem("p_taken")
        x0_added = sem("x0_added")
        p_stored = sems("p_stored", 2)
        zeroed = sem("zeroed")
        pick1_loaded = sems("pick1_loaded", RING)
        got1 = sems("got1_", RING)
        turn = sem("turn")
        rows_t = sem("rows_t")
        hot_ready = sem("hot_ready")
        hist_added = sem("hist_added")
        hist_done = sem("hist_done")
        scanned1 = sem("scanned1")
        back1 = sem("back1")
        copied1 = sem("copied1")
        stored1 = sems("stored1_", RING)
        seg_step = sem("seg_step")
        before_made = sem("before_made")
        seg_moved = sem("seg_moved")
        rows_known = sem("rows_known")
        carry_loaded = sem("carry_loaded")
        agg1_got = sems("agg1_got", NG)
        node_step = sem("node_step")
        agg1_ready = sem("agg1_ready")
        agg1_turned = sem("agg1_turned")
        agg1_t_ready = sem("agg1_t_ready")
        gin_done = sem("gin_done")
        x1_ready = sem("x1_ready")
        prod1 = sem("prod1")
        ab_taken = sem("ab_taken")
        y_taken = sem("y_taken")
        b_stored = sem("b_stored")
        seeded = sem("seeded")
        pick2_loaded = sems("pick2_loaded", RING)
        got2 = sems("got2_", RING)
        edges_loaded = sems("edges_loaded", RING)
        seeds_loaded = sems("seeds_loaded", RING)
        seeds_t = sem("seeds_t")
        filled2 = sem("filled2")
        summed = sem("summed")
        pre_ready = sem("pre_ready")
        relued = sem("relued")
        scanned2 = sem("scanned2")
        back2 = sem("back2")
        copied2 = sem("copied2")
        stored2 = sems("stored2_", RING)
        agg2_got = sems("agg2_got", NG)
        agg2_ready = sem("agg2_ready")
        agg2_turned = sem("agg2_turned")
        agg2_t_ready = sem("agg2_t_ready")
        out_prod = sem("out_prod")
        out_pre = sem("out_pre")
        out_relu = sem("out_relu")
        out_ready = sem("out_ready")
        out_stored = sem("out_stored")

        max_rows_half = max_rows.rearrange("r (h f) -> (r h) f", h=2)
        block = ctx.enter_context(nc.Block())

        @block.sync
        def _(sp):
            x_v = x.rearrange("(t p) f -> p t f", p=P)
            for q in range(NG):
                sp.dma_start(xs[:, q * TG:(q + 1) * TG, :],
                             x_v[:, q * TG:(q + 1) * TG, :]).then_inc(x_loaded[q], 16)
                if q == 0:
                    sp.dma_start(w0[:, 0:FE], w_fs).then_inc(w0_loaded, 16)
                    sp.dma_start(w0[:, FE:], w_gn).then_inc(w0_loaded, 16)
                    sp.dma_start(bias0[0:1, 0:FE], b_fs.unsqueeze(0)).then_inc(w0_loaded, 16)
                    sp.dma_start(bias_in[0:1, 0:F], b_gn.unsqueeze(0)).then_inc(w0_loaded, 16)
                    sp.dma_start(bias_in[0:1, F:], b_gin.unsqueeze(0)).then_inc(w0_loaded, 16)
                if q == 1:
                    sp.dma_start(dst_now[:, :], dst[:, 1:EPAD + 1].rearrange("o (p c) -> (o p) c", p=P)).then_inc(dst_loaded, 16)
                    sp.dma_start(dst_before[:, :], dst[:, 0:EPAD].rearrange("o (p c) -> (o p) c", p=P)).then_inc(dst_loaded, 16)
            sp.dma_start(mid_i[:, :], dst[0:1, HALF:HALF + 1].to_broadcast([P, 1])).then_inc(mid_loaded, 16)
            sp.dma_start(wgin[:, :], w_gin).then_inc(w12_loaded, 16)
            sp.dma_start(w1[:, :, :], w1_t.rearrange("(b p) f -> p b f", p=P)).then_inc(w12_loaded, 16)
            sp.dma_start(w2[:, :, :], w2_t.rearrange("(b p) f -> p b f", p=P)).then_inc(w12_loaded, 16)
            sp.dma_start(u0[:, :], u[0:1, :].rearrange("o f -> f o"), allow_slow_non_contiguous=True).then_inc(w12_loaded, 16)
            sp.dma_start(b12[0:1, 0:F], b1.unsqueeze(0)).then_inc(w12_loaded, 16)
            sp.dma_start(b12[0:1, F:], b2.unsqueeze(0)).then_inc(w12_loaded, 16)

            sp.wait_ge(same_made, 1)
            sp.dma_start(same_dram.rearrange("o (p c) -> (o p) c", p=P), same_row[:, :]).then_inc(same_stored, 16)
            sp.wait_ge(same_stored, 16)
            for half in range(2):
                sp.dma_start(same1[half * FE:(half + 1) * FE, :],
                             same_dram[0:1, half * HALF:(half + 1) * HALF].to_broadcast([FE, HALF])).then_inc(same1_loaded, 16)

            seed_blocks = seed_rows.rearrange("(g p r) f -> g p (r f)", p=P, r=2 * TPC)
            sp.wait_ge(consts, 1)

            def feed1(i, k):
                g = RING * i + k
                if not isinstance(i, int):
                    sp.wait_ge(got1[k], 16 * 2 * TPC * i)
                sp.dma_start(pick[:, k, :], src1[bass.ds(g, 1), :, :].rearrange("o p c -> (o p) c")
                             ).then_inc(pick1_loaded[k], 16)
                sp.dma_start(seed_blocks[bass.ds(g, 1), :, :].rearrange("o p c -> (o p) c"), zeros[:, :]
                             ).then_inc(zeroed, 16)

            for k in range(RING):
                feed1(0, k)
            with sp.Fori(1, NCH1 // RING) as i:
                for k in range(RING):
                    feed1(i, k)

            sp.dma_start(same2[:, :], same_dram[0:1, :].to_broadcast([P, EPAD])).then_inc(same2_loaded, 16)
            for k in range(RING):
                sp.wait_ge(stored1[k], 16 * (NCH1 // RING))
            sp.dma_start(carry[:, :], max_rows[HALF - 1:HALF, 0:FE].to_broadcast([P, FE])).then_inc(carry_loaded, 16)

            b_v = b_tab.rearrange("(t p) f -> p t f", p=P)
            for q in range(NG):
                sp.wait_ge(ab_taken, (q + 1) * TG)
                sp.dma_start(b_v[:, q * TG:(q + 1) * TG, :], ab[:, q * TG:(q + 1) * TG, F:2 * F]
                             ).then_inc(b_stored, 16)

            seed_chunks = seed_rows.rearrange("(c p r) f -> c p (r f)", p=P, r=TPC)

            def feed2(i, k):
                c = RING * i + k
                if isinstance(i, int):
                    sp.wait_ge(got1[k], 16 * 2 * TPC * (NCH1 // RING))
                else:
                    sp.wait_ge(got2[k], 16 * TPC * i)
                sp.dma_start(pick[:, k, 0:TPC], src2[bass.ds(c, 1), :, :].rearrange("o p c -> (o p) c")
                             ).then_inc(pick2_loaded[k], 16)
                if not isinstance(i, int):
                    sp.wait_ge(summed, c - RING + 1)
                sp.dma_start(edges[:, k, :], edge_t[bass.ds(c, 1), :, :].rearrange("o p c -> (o p) c")
                             ).then_inc(edges_loaded[k], 16)
                if isinstance(i, int) and k == 0:
                    sp.wait_ge(seeded, 16 * NT)
                sp.dma_start(seeds[:, k, :, :].rearrange("p r f -> p (r f)"),
                             seed_chunks[bass.ds(c, 1), :, :].rearrange("o p c -> (o p) c")
                             ).then_inc(seeds_loaded[k], 16)

            for k in range(RING):
                feed2(0, k)
            with sp.Fori(1, NCH // RING) as i:
                for k in range(RING):
                    feed2(i, k)

            for q in range(NG):
                sp.wait_ge(out_ready, q + 1)
                r0, r1 = q * TG * P, min((q + 1) * TG * P, N_NODES)
                full = (r1 - r0) // P
                sp.dma_start(out[r0:r0 + full * P, :].rearrange("(t p) f -> p t f", p=P),
                             ys[:, q * TG:q * TG + full, :]).then_inc(out_stored, 16)
                if r1 - r0 > full * P:
                    sp.dma_start(out[r0 + full * P:r1, :], ys[0:r1 - r0 - full * P, q * TG + full, :]
                                 ).then_inc(out_stored, 16)
            sp.wait_ge(out_stored, 16 * (NG + (N_NODES % P > 0)))

        @block.gpsimd
        def _(pool):
            nc.gpsimd.memset(ident[:, :], 1.0).then_inc(s_pool, 1)
            nc.gpsimd.memset(below[:, :], 1.0).then_inc(s_pool, 1)
            nc.gpsimd.iota(iota_i[:, :], [[1, P]], base=0, channel_multiplier=0)
            nc.gpsimd.iota(node_i[:, :], [[P, NT]], base=0, channel_multiplier=1).then_inc(iota_ready, 1)
            nc.gpsimd.memset(zeros[:, :], 0.0)
            nc.gpsimd.memset(zeros_bf[:, :], 0.0)
            pool.wait_ge(s_pool, 2)
            nc.gpsimd.affine_select(out=ident[:, :], in_=ident[:, :], compare_op=ALU.is_equal, fill=0.0,
                                    base=0, pattern=[[1, P]], channel_multiplier=-1).then_inc(s_pool, 1)
            nc.gpsimd.affine_select(out=below[:, :], in_=below[:, :], compare_op=ALU.is_gt, fill=0.0,
                                    base=0, pattern=[[1, P]], channel_multiplier=-1).then_inc(s_pool, 1)
            pool.wait_ge(s_pool, 4)
            nc.gpsimd.drain().then_inc(consts, 1)

            for b in range(2):
                pool.wait_ge(p_stored[b], 16 * ((NG + 1 - b) // 2))

            def gather1(i, k):
                g = RING * i + k
                pool.wait_ge(pick1_loaded[k], 16 * i + 16)
                if not isinstance(i, int):
                    pool.wait_ge(rows_t, g - RING + 1)
                pool.sem_inc(turn, 1)
                for j in range(TPC):
                    for half in range(2):
                        nc.gpsimd.indirect_dma_start(
                            out=rows[:, k, j, half * FE:(half + 1) * FE], out_offset=None, in_=p_tab[:, :],
                            in_offset=bass.IndirectOffsetOnAxis(ap=pick[:, k, 2 * j + half:2 * j + half + 1], axis=0),
                        ).then_inc(got1[k], 16)

            for k in range(RING):
                gather1(0, k)
            with pool.Fori(1, NCH1 // RING) as i:
                for k in range(RING):
                    gather1(i, k)

            pool.wait_ge(rows_known, 1)
            for k in range(RING):
                pool.wait_ge(stored1[k], 16 * (NCH1 // RING))
            for t in range(NT):
                nc.gpsimd.indirect_dma_start(
                    out=agg1[:, t, :], out_offset=None, in_=max_rows_half[:, :],
                    in_offset=bass.IndirectOffsetOnAxis(ap=max_at[:, t:t + 1], axis=0),
                ).then_inc(agg1_got[t // TG], 16)
            pool.wait_ge(zeroed, 16 * NCH1)
            for t in range(NT):
                pool.wait_ge(ab_taken, t + 1)
                nc.gpsimd.indirect_dma_start(
                    out=seed_rows[:, :], out_offset=bass.IndirectOffsetOnAxis(ap=seed_at[:, t:t + 1], axis=0),
                    in_=ab[:, t, 0:F], in_offset=None, bounds_check=EPAD - 1, oob_is_err=False,
                ).then_inc(seeded, 16)

            pool.wait_ge(b_stored, 16 * NG)

            def gather2(i, k):
                c = RING * i + k
                pool.wait_ge(pick2_loaded[k], 16 * i + 16)
                if not isinstance(i, int):
                    pool.wait_ge(summed, c - RING + 1)
                else:
                    pool.wait_ge(rows_t, NCH1)
                pool.sem_inc(turn, 1)
                for j in range(TPC):
                    nc.gpsimd.indirect_dma_start(
                        out=rows[:, k, j, :], out_offset=None, in_=b_tab[:, :],
                        in_offset=bass.IndirectOffsetOnAxis(ap=pick[:, k, j:j + 1], axis=0),
                    ).then_inc(got2[k], 16)

            for k in range(RING):
                gather2(0, k)
            with pool.Fori(1, NCH // RING) as i:
                for k in range(RING):
                    gather2(i, k)

            for k in range(RING):
                pool.wait_ge(stored2[k], 16 * (NCH // RING))
            pool.wait_ge(b_stored, 16 * NG)
            for t in range(NT):
                nc.gpsimd.indirect_dma_start(
                    out=agg2[:, t, 0:F], out_offset=None, in_=sum_rows[:, :],
                    in_offset=bass.IndirectOffsetOnAxis(ap=last_at[:, t:t + 1], axis=0),
                ).then_inc(agg2_got[t // TG], 16)

        @block.scalar
        def _(act):
            def norm_relu(q, phase):
                n = phase * NG + q
                act.wait_ge(var_done, n + 1)
                if n == 0:
                    act.wait_ge(dve_consts, 1)
                nc.scalar.activation(std[:, q * TG:(q + 1) * TG], mv[:, q * TG:(q + 1) * TG, 1], ACT.Sqrt,
                                     bias=eps[:, 0:1]).then_inc(std_done, 1)
                act.wait_ge(norm_ready, n + 1)
                if n >= 2:
                    act.wait_ge(ht_made, n - 1)
                for t in range(TG):
                    tt = q * TG + t
                    last = nc.scalar.activation(h[:, n % 2, t, :], xs[:, tt, :], ACT.Relu,
                                                bias=shift[:, tt:tt + 1], scale=rstd[:, tt:tt + 1])
                last.then_inc(h_ready, 1)

            def copy_ht(q, phase):
                n = phase * NG + q
                act.wait_ge(ht_made, n + 1)
                nc.scalar.copy(ht[:, n % 2, :, :].rearrange("p t f -> p (t f)"), ps[2][:, 0:TG * P]
                               ).then_inc(ht_ready, 1)

            def relu_p(q):
                if q >= 2:
                    act.wait_ge(p_stored[q % 2], 16 * (q // 2))
                for t in range(TG):
                    act.wait_ge(prod0, q * TG + t + 1)
                    nc.scalar.activation(p_out[:, q % 2, t, :], bank[6 + (q * TG + t) % 2][:, 0:FE], ACT.Relu
                                         ).then_inc(p_taken, 1)
                act.wait_ge(p_taken, (q + 1) * TG)
                act.dma_start(p_tab.rearrange("(t p) f -> p t f", p=P)[:, q * TG:(q + 1) * TG, :],
                              p_out[:, q % 2, :, :]).then_inc(p_stored[q % 2], 16)

            for q in range(NG):
                norm_relu(q, 0)
                copy_ht(q, 0)
                relu_p(q)

            max_chunks = max_rows.rearrange("(g p r) f -> g p (r f)", p=P, r=TPC)

            def store1(i, k):
                g = RING * i + k
                act.wait_ge(back1, g + 1)
                if not isinstance(i, int):
                    act.wait_ge(stored1[k], 16 * i)
                nc.scalar.copy(back[:, k, :], bank[2 + k % 2]).then_inc(copied1, 1)
                act.wait_ge(copied1, g + 1)
                act.dma_start(max_chunks[bass.ds(g, 1), :, :].rearrange("o p c -> (o p) c"), back[:, k, :]
                              ).then_inc(stored1[k], 16)

            for k in range(RING):
                store1(0, k)
            with act.Fori(1, NCH1 // RING) as i:
                for k in range(RING):
                    store1(i, k)

            for q in range(NG):
                act.wait_ge(agg1_turned, q + 1)
                nc.scalar.copy(agg1_t[:, q % 2, :, :].rearrange("p t f -> p (t f)"), ps[0][0:FE, 0:TG * P]
                               ).then_inc(agg1_t_ready, 1)
                norm_relu(q, 1)
                copy_ht(q, 1)
                for t in range(TG):
                    tt = q * TG + t
                    act.wait_ge(prod1, tt + 1)
                    nc.scalar.copy(ab[:, tt, :], bank[6 + tt % 2][:, 0:2 * F]).then_inc(ab_taken, 1)

            sum_chunks = sum_rows.rearrange("(c p r) f -> c p (r f)", p=P, r=TPC)

            def relu2(i, k):
                c = RING * i + k
                act.wait_ge(pre_ready, c + 1)
                nc.scalar.activation(msg[:, k % 2, :], msg[:, k % 2, :], ACT.Relu).then_inc(relued, 1)

            def store2(i, k):
                c = RING * i + k
                act.wait_ge(back2, c + 1)
                if not isinstance(i, int) or i > 0:
                    act.wait_ge(stored2[k], 16 * i)
                nc.scalar.copy(back[:, k, :], bank[4 + k % 2]).then_inc(copied2, 1)
                act.wait_ge(copied2, c + 1)
                act.dma_start(sum_chunks[bass.ds(c, 1), :, :].rearrange("o p c -> (o p) c"), back[:, k, :]
                              ).then_inc(stored2[k], 16)

            for k in range(RING):
                relu2(0, k)
                if k > 0:
                    store2(0, k - 1)
            with act.Fori(1, NCH // RING) as i:
                for k in range(RING):
                    relu2(i, k)
                    store2(i if k else i - 1, (k - 1) % RING)
            store2(NCH // RING - 1, RING - 1)

            for q in range(NG):
                act.wait_ge(agg2_turned, q + 1)
                nc.scalar.copy(ht[:, q % 2, :, :].rearrange("p t f -> p (t f)"), ps[3][:, 0:TG * P]
                               ).then_inc(agg2_t_ready, 1)
                act.wait_ge(out_pre, q + 1)
                g0, g1 = q * TG, (q + 1) * TG
                nc.scalar.activation(ys[:, g0:g1, :], ys[:, g0:g1, :], ACT.Relu).then_inc(out_relu, 1)

        @block.vector
        def _(dve):
            nc.vector.memset(eps[:, :], EPS)
            nc.vector.memset(ones[:, :], 1.0)
            nc.vector.memset(fill[:, 1, CH - 1:CH], 0.0)
            nc.vector.memset(scan[:, 1, CH - 1:CH], 0.0)
            nc.vector.memset(bias_aby[:, :], 0.0).then_inc(dve_consts, 1)
            dve.wait_ge(w0_loaded, 16 * 5)
            nc.vector.tensor_tensor(bias0[0:1, FE:], bias_in[0:1, 0:F], bias_in[0:1, F:], ALU.add
                                    ).then_inc(bias0_ready, 1)

            def norm_stats(q, phase):
                n = phase * NG + q
                for t in range(TG):
                    tt = q * TG + t
                    last = nc.vector.bn_stats(stats[:, tt, :], xs[:, tt, :])
                last.then_inc(stats_done, 1)
                dve.wait_ge(stats_done, n + 1)
                for t in range(TG):
                    tt = q * TG + t
                    last = nc.vector.bn_aggr(mv[:, tt, :], stats[:, tt, :])
                last.then_inc(var_done, 1)

            def norm_scale(q, phase):
                n = phase * NG + q
                g0, g1 = q * TG, (q + 1) * TG
                dve.wait_ge(std_done, n + 1)
                nc.vector.reciprocal(rstd[:, g0:g1], std[:, g0:g1]).then_inc(rstd_done, 1)
                dve.wait_ge(rstd_done, n + 1)
                nc.vector.scalar_tensor_tensor(out=shift[:, g0:g1], in0=mv[:, g0:g1, 0], scalar=-1.0,
                                               in1=rstd[:, g0:g1], op0=ALU.mult, op1=ALU.mult
                                               ).then_inc(norm_ready, 1)

            def add_x0(q):
                for t in range(TG):
                    tt = q * TG + t
                    dve.wait_ge(p_taken, tt + 1)
                    dve.wait_ge(h_ready, q + 1)
                    nc.vector.tensor_tensor(xs[:, tt, :], xs[:, tt, :], bank[6 + tt % 2][:, FE:FE + F], ALU.add
                                            ).then_inc(x0_added, 1)

            for q in range(NG):
                dve.wait_ge(x_loaded[q], 16)
                norm_stats(q, 0)
                if q > 0:
                    add_x0(q - 1)
                norm_scale(q, 0)
            dve.wait_ge(dst_loaded, 32)
            nc.vector.tensor_tensor(same_row[:, :], dst_now[:, :], dst_before[:, :], ALU.is_equal).then_inc(same_made, 1)
            nc.vector.tensor_scalar(dst_hi_i[:, :], dst_now[:, :], 7, None, ALU.arith_shift_right)
            nc.vector.tensor_scalar(dst_lo_i[:, :], dst_now[:, :], P - 1, None, ALU.bitwise_and).then_inc(split_dst, 1)
            dve.wait_ge(split_dst, 1)
            nc.vector.tensor_copy(dst_hi[:, :], dst_hi_i[:, :])
            nc.vector.tensor_copy(dst_lo[:, :], dst_lo_i[:, :])
            dve.wait_ge(iota_ready, 1)
            nc.vector.tensor_copy(iota_bf[:, :], iota_i[:, :])
            nc.vector.tensor_copy(node_f[:, :], node_i[:, :])
            dve.wait_ge(mid_loaded, 16)
            nc.vector.tensor_copy(mid_f[:, :], mid_i[:, :]).then_inc(split_dst, 1)
            add_x0(NG - 1)
            dve.wait_ge(split_dst, 2)
            nc.vector.tensor_scalar(is_mid[:, :], node_f[:, :], mid_f[:, 0:1], None, ALU.is_equal)
            dve.wait_ge(w12_loaded, 16 * 6)
            nc.vector.tensor_copy(w_aby[:, 0:2 * F].rearrange("p (b f) -> p b f", b=2), w1[:, 0:2, :])
            nc.vector.tensor_copy(w_aby[:, 2 * F:], w2[:, 0, :]).then_inc(w_aby_ready, 1)
            dve.wait_ge(bias_made, 1)
            nc.vector.tensor_tensor(bias_aby[0:1, 0:F], bias_ps[:, 0:F], b12[0:1, 0:F], ALU.add)
            nc.vector.tensor_tensor(bias_aby[0:1, 2 * F:], bias_ps[:, F:], b12[0:1, F:], ALU.add
                                    ).then_inc(bias_aby_ready, 1)

            def scan1(i, k):
                g = RING * i + k
                peeled = isinstance(i, int)
                if not peeled or k >= 2:
                    dve.wait_ge(hist_added, g - 1)
                nc.vector.tensor_tensor(hot_hi[:, k % 2, :, :],
                                        dst_hi[:, bass.ds(HC * g, HC)].unsqueeze(2).to_broadcast([P, HC, NT]),
                                        iota_bf[:, 0:NT].unsqueeze(1).to_broadcast([P, HC, NT]), ALU.is_equal)
                nc.vector.tensor_tensor(hot_lo[:, k % 2, :, :],
                                        dst_lo[:, bass.ds(HC * g, HC)].unsqueeze(2).to_broadcast([P, HC, P]),
                                        iota_bf[:, :].unsqueeze(1).to_broadcast([P, HC, P]), ALU.is_equal
                                        ).then_inc(hot_ready, 1)
                if not peeled or k > 0:
                    dve.wait_ge(scanned1, g)
                if not peeled or k >= 2:
                    dve.wait_ge(back1, g - 1)
                dve.wait_ge(rows_t, g + 1)
                nc.vector.tensor_tensor_scan(scan[:, k % 2, :], same1[:, bass.ds(CH * g, CH)], bank[k % 2],
                                             scan[:, (k + 1) % 2, CH - 1:CH], ALU.mult, ALU.max
                                             ).then_inc(scanned1, 1)

            dve.wait_ge(same1_loaded, 32)
            for k in range(RING):
                scan1(0, k)
            with dve.Fori(1, NCH1 // RING) as i:
                for k in range(RING):
                    scan1(i, k)

            step = [0]

            def link(ins):
                step[0] += 1
                ins.then_inc(seg_step, 1)
                dve.wait_ge(seg_step, step[0])

            dve.wait_ge(hist_done, 1)
            link(nc.vector.tensor_copy(count[:, :], hist))
            link(nc.vector.tensor_tensor_scan(upto[:, :], zeros_bf[0:NT, :], count[:, :], 0.0, ALU.add, ALU.add))
            dve.wait_ge(before_made, 1)
            link(nc.vector.tensor_copy(before[:, :], before_ps))
            link(nc.vector.tensor_scalar(end_row[:, :], upto[:, :], before[:, 0:1], None, ALU.add))
            dve.wait_ge(seg_moved, 1)
            nc.vector.tensor_copy(seg_end[:, :], seg_ps[:, 0:NT])
            link(nc.vector.tensor_copy(seg_count[:, :], seg_ps[:, NT:]))
            nc.vector.tensor_scalar(empty[:, :], seg_count[:, :], 0.0, None, ALU.is_equal)
            nc.vector.tensor_scalar(filled[:, :], seg_count[:, :], 0.0, None, ALU.is_gt)
            link(nc.vector.tensor_scalar(last_f[:, :], seg_end[:, :], -1.0, 0.0, ALU.add, ALU.max))
            link(nc.vector.tensor_scalar(upper[:, :], last_f[:, :], float(HALF), float(1 - EPAD), ALU.is_ge, ALU.mult))
            link(nc.vector.scalar_tensor_tensor(out=max_at_f[:, :], in0=last_f[:, :], scalar=2.0, in1=upper[:, :],
                                                op0=ALU.mult, op1=ALU.add))
            nc.vector.tensor_copy(last_at[:, :], last_f[:, :])
            link(nc.vector.tensor_copy(max_at[:, :], max_at_f[:, :]))
            nc.vector.engine_nop().then_inc(rows_known, 1)
            link(nc.vector.tensor_tensor(seed_at_f[:, :], seg_end[:, :], seg_count[:, :], ALU.subtract))
            link(nc.vector.scalar_tensor_tensor(out=seed_at_f[:, :], in0=empty[:, :], scalar=float(SKIP),
                                                in1=seed_at_f[:, :], op0=ALU.mult, op1=ALU.add))
            link(nc.vector.tensor_copy(seed_at[:, :], seed_at_f[:, :]))
            dve.wait_ge(carry_loaded, 16)
            link(nc.vector.tensor_tensor(carried[:, :, :], carry[:, :].unsqueeze(1).to_broadcast([P, NT, FE]),
                                         is_mid[:, :].unsqueeze(2).to_broadcast([P, NT, FE]), ALU.mult))

            nstep = [0]

            def nlink(ins):
                nstep[0] += 1
                ins.then_inc(node_step, 1)
                dve.wait_ge(node_step, nstep[0])

            for q in range(NG):
                g0, g1 = q * TG, (q + 1) * TG
                dve.wait_ge(agg1_got[q], 16 * TG)
                nlink(nc.vector.tensor_tensor(agg1[:, g0:g1, :], agg1[:, g0:g1, :],
                                              filled[:, g0:g1].unsqueeze(2).to_broadcast([P, TG, FE]), ALU.mult))
                nc.vector.tensor_tensor(agg1[:, g0:g1, :], agg1[:, g0:g1, :], carried[:, g0:g1, :], ALU.max
                                        ).then_inc(agg1_ready, 1)
                dve.wait_ge(gin_done, q + 1)
                nlink(nc.vector.tensor_tensor(xs[:, g0:g1, :].rearrange("p t f -> p (t f)"),
                                              xs[:, g0:g1, :].rearrange("p t f -> p (t f)"),
                                              ps[1][:, 0:TG * F], ALU.add))
                nc.vector.engine_nop().then_inc(x1_ready, 1)
                norm_stats(q, 1)
                norm_scale(q, 1)
                for t in range(TG):
                    tt = g0 + t
                    dve.wait_ge(ab_taken, tt + 1)
                    nc.vector.tensor_copy(ys[:, tt, :], bank[6 + tt % 2][:, 2 * F:3 * F]).then_inc(y_taken, 1)

            def front2(i, k):
                c = RING * i + k
                peeled = isinstance(i, int)
                dve.wait_ge(seeds_t, c + 1)
                if not peeled or k > 0:
                    dve.wait_ge(filled2, c)
                nc.vector.tensor_tensor_scan(fill[:, k % 2, :], same2[:, bass.ds(CH * c, CH)], bank[k % 2],
                                             fill[:, (k + 1) % 2, CH - 1:CH], ALU.mult, ALU.add
                                             ).then_inc(filled2, 1)
                dve.wait_ge(summed, c + 1)
                dve.wait_ge(filled2, c + 1)
                if not peeled or k >= 2:
                    dve.wait_ge(scanned2, c - 1)
                nc.vector.tensor_tensor(msg[:, k % 2, :], fill[:, k % 2, :], bank[2 + k % 2], ALU.add
                                        ).then_inc(pre_ready, 1)

            def scan2(i, k):
                c = RING * i + k
                peeled = isinstance(i, int) and i == 0
                dve.wait_ge(relued, c + 1)
                if not peeled or k > 0:
                    dve.wait_ge(scanned2, c)
                if not peeled or k >= 2:
                    dve.wait_ge(back2, c - 1)
                nc.vector.tensor_tensor_scan(scan[:, k % 2, :], same2[:, bass.ds(CH * c, CH)], msg[:, k % 2, :],
                                             scan[:, (k + 1) % 2, CH - 1:CH], ALU.mult, ALU.add
                                             ).then_inc(scanned2, 1)

            dve.wait_ge(same2_loaded, 16)
            for k in range(RING):
                front2(0, k)
                if k > 0:
                    scan2(0, k - 1)
            with dve.Fori(1, NCH // RING) as i:
                for k in range(RING):
                    front2(i, k)
                    scan2(i if k else i - 1, (k - 1) % RING)
            scan2(NCH // RING - 1, RING - 1)

            for q in range(NG):
                g0, g1 = q * TG, (q + 1) * TG
                dve.wait_ge(agg2_got[q], 16 * TG)
                nc.vector.tensor_tensor(agg2[:, g0:g1, 0:F], agg2[:, g0:g1, 0:F],
                                        filled[:, g0:g1].unsqueeze(2).to_broadcast([P, TG, F]), ALU.mult
                                        ).then_inc(agg2_ready, 1)
                dve.wait_ge(out_prod, q + 1)
                nc.vector.tensor_tensor(ys[:, g0:g1, :].rearrange("p t f -> p (t f)"),
                                        ys[:, g0:g1, :].rearrange("p t f -> p (t f)"),
                                        ps[0][:, 0:TG * F], ALU.add).then_inc(out_pre, 1)
                dve.wait_ge(out_relu, q + 1)
                nc.vector.tensor_tensor(ys[:, g0:g1, :], ys[:, g0:g1, :], xs[:, g0:g1, :], ALU.add
                                        ).then_inc(out_ready, 1)

        @block.tensor
        def _(pe):
            def turn_h(q, phase):
                n = phase * NG + q
                pe.wait_ge(h_ready, n + 1)
                if n > 0:
                    pe.wait_ge(ht_ready, n)
                for t in range(TG):
                    last = nc.tensor.transpose(ps[2][:, t * P:(t + 1) * P], h[:, n % 2, t, :], ident[:, :])
                last.then_inc(ht_made, 1)

            pe.wait_ge(consts, 1)
            pe.wait_ge(dve_consts, 1)
            for q in range(NG):
                turn_h(q, 0)
                pe.wait_ge(ht_ready, q + 1)
                if q == 0:
                    pe.wait_ge(bias0_ready, 1)
                for t in range(TG):
                    tt = q * TG + t
                    if tt >= 2:
                        pe.wait_ge(p_taken, tt - 1)
                        pe.wait_ge(x0_added, tt - 1)
                    dst_ps = bank[6 + tt % 2][:, 0:FE + F]
                    nc.tensor.matmul(dst_ps, ones[0:1, :], bias0[0:1, :], start=True, stop=False)
                    nc.tensor.matmul(dst_ps, ht[:, q % 2, t, :], w0[:, :], start=False, stop=True).then_inc(prod0, 1)
            pe.wait_ge(w12_loaded, 16 * 6)
            nc.tensor.matmul(bias_ps[:, 0:F], u0[:, 0:1], w1[:, 3, :], start=True, stop=True)
            nc.tensor.matmul(bias_ps[:, F:], u0[:, 0:1], w2[:, 2, :], start=True, stop=True).then_inc(bias_made, 1)

            pe.wait_ge(ht_ready, NG)
            nc.tensor.matmul(hist, zeros_bf[:, 0:NT], zeros_bf[:, :], start=True, stop=False)

            def turn1(i, k):
                g = RING * i + k
                peeled = isinstance(i, int)
                pe.wait_ge(got1[k], 16 * 2 * TPC * (i + 1))
                if not peeled or k >= 2:
                    pe.wait_ge(scanned1, g - 1)
                for j in range(TPC):
                    last = nc.tensor.transpose(bank[k % 2][:, j * P:(j + 1) * P], rows[:, k, j, :], ident[:, :])
                last.then_inc(rows_t, 1)
                pe.wait_ge(hot_ready, g + 1)
                for j in range(HC):
                    last = nc.tensor.matmul(hist, hot_hi[:, k % 2, j, :], hot_lo[:, k % 2, j, :], start=False,
                                            stop=False)
                last.then_inc(hist_added, 1)
                pe.wait_ge(scanned1, g + 1)
                if not peeled or k >= 2:
                    pe.wait_ge(copied1, g - 1)
                for j in range(TPC):
                    last = nc.tensor.transpose(bank[2 + k % 2][:, j * P:(j + 1) * P], scan[:, k % 2, j::TPC],
                                               ident[:, :])
                last.then_inc(back1, 1)

            for k in range(RING):
                turn1(0, k)
            with pe.Fori(1, NCH1 // RING) as i:
                for k in range(RING):
                    turn1(i, k)
            nc.tensor.matmul(hist, zeros_bf[:, 0:NT], zeros_bf[:, :], start=False, stop=True).then_inc(hist_done, 1)

            pe.wait_ge(seg_step, 2)
            nc.tensor.matmul(before_ps, below[0:NT, 0:NT], upto[:, P - 1:P], start=True, stop=True).then_inc(before_made, 1)
            pe.wait_ge(seg_step, 4)
            nc.tensor.transpose(seg_ps[:, 0:NT], end_row[:, :], ident[0:NT, 0:NT])
            nc.tensor.transpose(seg_ps[:, NT:], count[:, :], ident[0:NT, 0:NT]).then_inc(seg_moved, 1)

            pe.wait_ge(copied1, NCH1)
            pe.wait_ge(seg_step, 5)
            pe.wait_ge(w_aby_ready, 1)
            pe.wait_ge(bias_aby_ready, 1)
            for q in range(NG):
                pe.wait_ge(agg1_ready, q + 1)
                if q > 0:
                    pe.wait_ge(agg1_t_ready, q)
                for t in range(TG):
                    last = nc.tensor.transpose(ps[0][0:FE, t * P:(t + 1) * P], agg1[:, q * TG + t, :], ident[:, :])
                last.then_inc(agg1_turned, 1)
                pe.wait_ge(agg1_t_ready, q + 1)
                if q > 0:
                    pe.wait_ge(x1_ready, q)
                for t in range(TG):
                    last = nc.tensor.matmul(ps[1][:, t * F:(t + 1) * F], agg1_t[:, q % 2, t, :], wgin[:, :],
                                            start=True, stop=True)
                last.then_inc(gin_done, 1)
                turn_h(q, 1)
                pe.wait_ge(ht_ready, NG + q + 1)
                for t in range(TG):
                    tt = q * TG + t
                    if tt >= 2:
                        pe.wait_ge(ab_taken, tt - 1)
                        pe.wait_ge(y_taken, tt - 1)
                    dst_ps = bank[6 + tt % 2][:, 0:3 * F]
                    nc.tensor.matmul(dst_ps, ones[0:1, :], bias_aby[0:1, :], start=True, stop=False)
                    nc.tensor.matmul(dst_ps, ht[:, (NG + q) % 2, t, :], w_aby[:, :], start=False, stop=True
                                     ).then_inc(prod1, 1)

            pe.wait_ge(x1_ready, NG)
            pe.wait_ge(ht_ready, 2 * NG)

            def front2(i, k):
                c = RING * i + k
                peeled = isinstance(i, int)
                pe.wait_ge(seeds_loaded[k], 16 * i + 16)
                if not peeled or k >= 2:
                    pe.wait_ge(filled2, c - 1)
                for j in range(TPC):
                    last = nc.tensor.transpose(bank[k % 2][:, j::TPC], seeds[:, k, j, :], ident[:, :])
                last.then_inc(seeds_t, 1)
                pe.wait_ge(edges_loaded[k], 16 * i + 16)
                if not peeled or k >= 2:
                    pe.wait_ge(pre_ready, c - 1)
                nc.tensor.matmul(bank[2 + k % 2], w1[:, 2, :], edges[:, k, :], start=True, stop=False)
                pe.wait_ge(got2[k], 16 * TPC * (i + 1))
                for j in range(TPC):
                    last = nc.tensor.matmul(bank[2 + k % 2][:, j * P:(j + 1) * P], rows[:, k, j, :], ident[:, :],
                                            start=False, stop=(j == TPC - 1))
                last.then_inc(summed, 1)

            def back_2(i, k):
                c = RING * i + k
                peeled = isinstance(i, int) and i == 0
                pe.wait_ge(scanned2, c + 1)
                if not peeled or k >= 2:
                    pe.wait_ge(copied2, c - 1)
                for j in range(TPC):
                    last = nc.tensor.transpose(bank[4 + k % 2][:, j * P:(j + 1) * P], scan[:, k % 2, j::TPC],
                                               ident[:, :])
                last.then_inc(back2, 1)

            for k in range(RING):
                front2(0, k)
                if k > 0:
                    back_2(0, k - 1)
            with pe.Fori(1, NCH // RING) as i:
                for k in range(RING):
                    front2(i, k)
                    back_2(i if k else i - 1, (k - 1) % RING)
            back_2(NCH // RING - 1, RING - 1)

            for q in range(NG):
                pe.wait_ge(agg2_ready, q + 1)
                if q > 0:
                    pe.wait_ge(agg2_t_ready, q)
                for t in range(TG):
                    last = nc.tensor.transpose(ps[3][:, t * P:(t + 1) * P], agg2[:, q * TG + t, 0:F], ident[:, :])
                last.then_inc(agg2_turned, 1)
                pe.wait_ge(agg2_t_ready, q + 1)
                if q > 0:
                    pe.wait_ge(out_pre, q)
                for t in range(TG):
                    last = nc.tensor.matmul(ps[0][:, t * F:(t + 1) * F], ht[:, q % 2, t, :], w2[:, 1, :],
                                            start=True, stop=True)
                last.then_inc(out_prod, 1)


def kernel(x, src, dst, edge_attr_128, L0_gnn_W_fs, L0_gnn_b_fs, L0_gnn_W_gn, L0_gnn_b_gn, L0_gnn_W_gin,
           L0_gnn_b_gin, L1_gnn_u, L1_gnn_W1, L1_gnn_b1, L1_gnn_W2, L1_gnn_b2):
    import numpy as np
    import concourse.bacc as bacc
    from concourse.bass_utils import run_bass_kernel_spmd

    x, src, dst, e = (np.asarray(a) for a in (x, src, dst, edge_attr_128))
    src_pad = np.concatenate([src, np.zeros(EPAD - N_EDGES, src.dtype)])
    e_pad = np.concatenate([e, np.zeros((EPAD - N_EDGES, F), e.dtype)])
    arrays = {
        "x": np.concatenate([x, np.zeros((NPAD - N_NODES, F), x.dtype)]),
        "src1": src_pad.reshape(2, NCH1, TPC, P).transpose(1, 3, 2, 0).reshape(NCH1, P, 2 * TPC),
        "src2": src_pad.reshape(NCH, TPC, P).transpose(0, 2, 1),
        "dst": np.concatenate([np.full(1, -1, dst.dtype), dst, np.full(EPAD - N_EDGES, DST_PAD, dst.dtype)])[None, :],
        "edge_t": e_pad.reshape(NCH, CH, F).transpose(0, 2, 1),
        "w_fs": L0_gnn_W_fs, "b_fs": L0_gnn_b_fs, "w_gn": L0_gnn_W_gn, "b_gn": L0_gnn_b_gn,
        "w_gin": L0_gnn_W_gin, "b_gin": L0_gnn_b_gin, "u": L1_gnn_u, "w1_t": np.asarray(L1_gnn_W1).T,
        "b1": L1_gnn_b1, "w2_t": np.asarray(L1_gnn_W2).T, "b2": L1_gnn_b2,
    }
    arrays = {"in_" + name: np.ascontiguousarray(a) for name, a in arrays.items()}
    nc = bacc.Bacc("TRN2", target_bir_lowering=False, num_devices=1)
    ins = [nc.dram_tensor(name, a.shape, mybir.dt.from_np(a.dtype), kind="ExternalInput").ap()
           for name, a in arrays.items()]
    out = nc.dram_tensor("out", (N_NODES, F), mybir.dt.float32, kind="ExternalOutput").ap()
    gnn_program(nc, *ins, out)
    r = run_bass_kernel_spmd(nc, [arrays], core_ids=[0])
    return r.results[0]["out"]
```

```python
import concourse.bass as bass
from concourse import mybir
from contextlib import ExitStack

N_NODES, N_EDGES, F, FE = 3125, 53125, 128, 64
P = 128
NT = -(-N_NODES // P)
NPAD = NT * P
TG = 4
GROUPS = [range(t, min(t + TG, NT)) for t in range(0, NT, TG)]
NG = len(GROUPS)
AHEAD = 2
CH = 512
TPC = CH // P
RING = 4
RING2 = 8
NCH = -(-N_EDGES // (CH * RING2)) * RING2
EPAD = NCH * CH
HALF = EPAD // 2
NCH1 = NCH // 2
EC = EPAD // P
TPG = TPC - 1
NSPLIT = 3
HC = EC // NCH1
EPS = 1e-5
DST_PAD = NPAD
MID = 2048
SKIP = 1 << 17


def gnn_program(nc, x, src1, src_hot, src2, dst, edge_t, w_fs, b_fs, w_gn, b_gn, w_gin, b_gin, u, w1_t, b1,
                w2_t, b2, out):
    fp32, bf16, i32, u8 = mybir.dt.float32, mybir.dt.bfloat16, mybir.dt.int32, mybir.dt.uint8
    fp16 = mybir.dt.float16
    ALU = mybir.AluOpType
    ACT = mybir.ActivationFunctionType

    with ExitStack() as ctx:
        def sb(name, shape, dt=fp32):
            return ctx.enter_context(nc.sbuf_tensor(name, shape, dt))

        def sem(name):
            return ctx.enter_context(nc.semaphore(name))

        def sems(name, n):
            return [sem(f"{name}{i}") for i in range(n)]

        p_tab = nc.dram_tensor("p_tab", (NPAD, FE), fp32).ap()
        b_tab = nc.dram_tensor("b_tab", (NPAD, F), fp32).ap()
        same_dram = nc.dram_tensor("same_dram", (1, EPAD), u8).ap()
        max_rows = nc.dram_tensor("max_rows", (HALF, 2 * FE), fp32).ap()
        seed_rows = nc.dram_tensor("seed_rows", (EPAD, F), fp32).ap()
        sum_rows = nc.dram_tensor("sum_rows", (EPAD, F), fp32).ap()

        ident = sb("ident", [P, P])
        below = sb("below", [P, P])
        iota_i = sb("iota_i", [P, P], i32)
        iota_bf = sb("iota_bf", [P, P], bf16)
        node_i = sb("node_i", [P, NT], i32)
        node_f = sb("node_f", [P, NT])
        node_m = sb("node_m", [P, NT])
        ident_bf = sb("ident_bf", [P, P], bf16)
        ident_h = sb("ident_h", [P, P], fp16)
        zeros_bf = sb("zeros_bf", [P, P], bf16)
        eps = sb("eps", [P, 1])
        w0 = sb("w0", [P, FE + F])
        wgin = sb("wgin", [FE, F])
        w1 = sb("w1", [P, 4, F])
        w2 = sb("w2", [P, 3, F])
        u0 = sb("u0", [P, 1])
        u0_wide = sb("u0_wide", [P, P])
        bias_p = sb("bias_p", [P, FE])
        bias_g2 = sb("bias_g2", [P, 2, F])
        bias_g = sb("bias_g", [P, F])
        bias_12 = sb("bias_12", [P, 2, F])
        bias_a = sb("bias_a", [P, F])
        bias_y = sb("bias_y", [P, F])

        xs = sb("xs", [P, NT, F])
        ht = sb("ht", [P, NT, F])
        stats = sb("stats", [P, NT, 6])
        mv = sb("mv", [P, NT, 2])
        std = sb("std", [P, NT])
        rstd = sb("rstd", [P, NT])
        shift = sb("shift", [P, NT])
        h = sb("h", [P, 2, TG, F])
        agg2_t = sb("agg2_t", [P, 2, TG, P])
        res = sb("res", [P, 2, TG, F])
        p_out = sb("p_out", [P, NT, FE])
        agg1 = p_out
        carry = sb("carry", [P, FE])
        carried = ht[:, :, 0:FE]
        agg1_t = sb("agg1_t", [FE, 2, TG, P])
        place = sb("place", [P, HALF], u8)
        same1 = place[:, :]
        ab = place[:, 0:4 * NT * 2 * F].bitcast(fp32).rearrange("p (t c) -> p t c", t=NT)
        agg2 = ab

        dst_hi = sb("dst_hi", [P, EC], bf16)
        dst_lo = sb("dst_lo", [P, EC], bf16)
        same_row = sb("same_row", [P, EC], u8)
        same2 = sb("same2", [P, EPAD], u8)
        sizes = [2 * NT * NSPLIT * FE, 2 * NT * P, 2 * 2 * NT * 2 * P, 4 * NT * FE]
        ends = [sum(sizes[:n + 1]) for n in range(len(sizes))]
        parts, node_wide, hot_src, rest = (same2[:, e - n:e].bitcast(dt)
                                           for e, n, dt in zip(ends, sizes, (bf16, fp16, bf16, fp32)))
        parts = parts.rearrange("p (t c) -> p t c", t=NT)
        node_wide = node_wide.rearrange("p (t e) -> p t e", t=NT)
        hot_src = hot_src.rearrange("p (k t h e) -> p k t h e", k=2, t=NT, h=2)
        rest = rest.rearrange("p (t f) -> p t f", t=NT)
        src_i = sb("src_i", [P, NCH1, 2], i32)
        src_m = sb("src_m", [P, 2, 2], fp16)
        row_parts = sb("row_parts", [P, 2, NSPLIT, 2, FE], bf16)
        hot_lo = sb("hot_lo", [P, 2, HC, P], bf16)
        hot_hi = sb("hot_hi", [P, 2, HC, NT], bf16)
        count = sb("count", [NT, P])
        upto = sb("upto", [NT, P])
        end_row = sb("end_row", [NT, P])
        before = sb("before", [NT, 1])
        seg_end = sb("seg_end", [P, NT])
        seg_count = sb("seg_count", [P, NT])
        empty = sb("empty", [P, NT])
        filled = sb("filled", [P, NT])
        last_f = sb("last_f", [P, NT])
        upper = sb("upper", [P, NT])
        max_at_f = sb("max_at_f", [P, NT])
        seed_at_f = sb("seed_at_f", [P, NT])
        last_at = sb("last_at", [P, NT], i32)
        max_at = sb("max_at", [P, NT], i32)
        seed_at = sb("seed_at", [P, NT], i32)
        mid_i = sb("mid_i", [P, 1], i32)
        mid_f = sb("mid_f", [P, 1])
        is_mid = sb("is_mid", [P, NT])

        pick = sb("pick", [P, RING2, 2 * TPC], i32)
        rows = sb("rows", [P, RING2, TPC, F])
        edges = sb("edges", [P, RING, CH])
        dst_now, dst_before, dst_hi_i, dst_lo_i = (edges[:, k, 0:EC].bitcast(i32) for k in range(RING))
        seeds = sb("seeds", [P, RING, TPC, F])
        zeros = seeds[:, 0:2, :, :].rearrange("p k r f -> p (k r f)")
        fill = sb("fill", [P, 2, CH])
        msg = sb("msg", [P, 2, CH])
        scan = sb("scan", [P, 2, CH])
        back = sb("back", [P, RING, CH])

        ps = [ctx.enter_context(nc.psum_tensor(f"ps{i}", [P, 2 * CH], fp32)) for i in range(4)]
        bank = [ps[i // 2][:, (i % 2) * CH:(i % 2 + 1) * CH] for i in range(8)]
        hist = bank[4][0:NT, 0:P]
        seg_ps = bank[4][:, P:P + 2 * NT]
        before_ps = bank[4][0:NT, 2 * P:2 * P + 1]
        bias_ps = bank[5][:, 0:2 * F]
        row_ps = bank[5][:, 0:2 * NSPLIT * FE]
        src_ps = [bank[6 + k][:, 0:P].bitcast(fp16).rearrange("p (h e) -> p h e", h=2) for k in range(2)]

        x_loaded = sems("x_loaded", NG)
        w0_loaded = sem("w0_loaded")
        w12_loaded = sem("w12_loaded")
        dst_loaded = sem("dst_loaded")
        mid_loaded = sem("mid_loaded")
        s_pool = sem("s_pool")
        consts = sem("consts")
        dve_consts = sem("dve_consts")
        iota_ready = sem("iota_ready")
        bias_made = sem("bias_made")
        bias_ready = sem("bias_ready")
        u0_ready = sem("u0_ready")
        p_made = sem("p_made")
        g_made = sem("g_made")
        p_pre = sem("p_pre")
        p_relued = sem("p_relued")
        x0_added = sem("x0_added")
        a_made = sem("a_made")
        b_made = sem("b_made")
        a_ready = sem("a_ready")
        b_ready = sem("b_ready")
        split_dst = sem("split_dst")
        same_made = sem("same_made")
        same_stored = sem("same_stored")
        same1_loaded = sem("same1_loaded")
        same2_loaded = sem("same2_loaded")
        stats_done = sem("stats_done")
        var_done = sem("var_done")
        std_done = sem("std_done")
        rstd_done = sem("rstd_done")
        norm_ready = sem("norm_ready")
        h_ready = sem("h_ready")
        ht_made = sem("ht_made")
        ht_ready = sem("ht_ready")
        p_stored = sem("p_stored")
        act_warm = sem("act_warm")
        node_m_ready = sem("node_m_ready")
        node_wide_ready = sem("node_wide_ready")
        idents_ready = sem("idents_ready")
        src_loaded = sem("src_loaded")
        hi_made = sem("hi_made")
        rest_made = sem("rest_made")
        mid_made = sem("mid_made")
        parts_ready = sem("parts_ready")
        staged = sem("staged")
        spread = sem("spread")
        hot_src_ready = sem("hot_src_ready")
        row_made = sem("row_made")
        row_split = sem("row_split")
        zeroed = sem("zeroed")
        pick1_loaded = sems("pick1_loaded", RING)
        got1 = sems("got1_", RING)
        turn = sem("turn")
        rows_t = sem("rows_t")
        hot_ready = sem("hot_ready")
        hist_added = sem("hist_added")
        hist_done = sem("hist_done")
        scanned1 = sem("scanned1")
        back1 = sem("back1")
        copied1 = sem("copied1")
        stored1 = sems("stored1_", RING)
        seg_step = sem("seg_step")
        before_made = sem("before_made")
        seg_moved = sem("seg_moved")
        rows_known = sem("rows_known")
        carry_loaded = sem("carry_loaded")
        agg1_got = sems("agg1_got", NG)
        node_step = sem("node_step")
        agg1_ready = sem("agg1_ready")
        agg1_turned = sem("agg1_turned")
        agg1_t_ready = sem("agg1_t_ready")
        gin_done = sem("gin_done")
        x1_ready = sem("x1_ready")
        b_stored = sem("b_stored")
        seeded = sem("seeded")
        pick2_loaded = sems("pick2_loaded", RING2)
        got2 = sems("got2_", RING2)
        edges_loaded = sems("edges_loaded", RING)
        seeds_loaded = sems("seeds_loaded", RING)
        seeds_t = sem("seeds_t")
        filled2 = sem("filled2")
        summed = sem("summed")
        pre_ready = sem("pre_ready")
        relued = sem("relued")
        scanned2 = sem("scanned2")
        back2 = sem("back2")
        copied2 = sem("copied2")
        stored2 = sems("stored2_", RING)
        agg2_got = sems("agg2_got", NG)
        agg2_ready = sem("agg2_ready")
        agg2_turned = sem("agg2_turned")
        agg2_t_ready = sem("agg2_t_ready")
        out_prod = sem("out_prod")
        out_pre = sem("out_pre")
        out_ready = sem("out_ready")
        out_stored = sem("out_stored")

        max_rows_half = max_rows.rearrange("r (h f) -> (r h) f", h=2)
        block = ctx.enter_context(nc.Block())

        @block.sync
        def _(sp):
            x_v = x.rearrange("(t p) f -> p t f", p=P)

            def load_row(to, row, done):
                sp.dma_start(to, row.unsqueeze(0).to_broadcast([P, to.shape[-1]])).then_inc(done, 16)

            for q, g in enumerate(GROUPS):
                sp.dma_start(xs[:, g.start:g.stop, :], x_v[:, g.start:g.stop, :]).then_inc(x_loaded[q], 16)
                if q == 0:
                    sp.dma_start(dst_now[:, :], dst[:, 1:EPAD + 1].rearrange("o (p c) -> (o p) c", p=P)
                                 ).then_inc(dst_loaded, 16)
                    sp.dma_start(dst_before[:, :], dst[:, 0:EPAD].rearrange("o (p c) -> (o p) c", p=P)
                                 ).then_inc(dst_loaded, 16)
                if q == 1:
                    sp.dma_start(w0[:, 0:FE], w_fs).then_inc(w0_loaded, 16)
                    load_row(bias_p[:, :], b_fs, w0_loaded)
                    sp.dma_start(w0[:, FE:], w_gn).then_inc(w0_loaded, 16)
            sp.dma_start(src_i[:, :, :].rearrange("p g h -> p (g h)"), src_hot).then_inc(src_loaded, 16)

            seed_blocks = seed_rows.rearrange("(g p r) f -> g p (r f)", p=P, r=2 * TPC)

            def feed1(i, k):
                g = RING * i + k
                if not isinstance(i, int):
                    sp.wait_ge(got1[k], 16 * 2 * TPG * i)
                sp.dma_start(pick[:, k, 0:2 * TPG], src1[bass.ds(g, 1), :, :].rearrange("o p c -> (o p) c")
                             ).then_inc(pick1_loaded[k], 16)

            def zero1(i, k):
                g = RING * i + k
                sp.dma_start(seed_blocks[bass.ds(g, 1), :, :].rearrange("o p c -> (o p) c"), zeros[:, :]
                             ).then_inc(zeroed, 16)

            for k in range(RING):
                feed1(0, k)

            sp.wait_ge(same_made, 1)
            sp.dma_start(same_dram.rearrange("o (p c) -> (o p) c", p=P), same_row[:, :]).then_inc(same_stored, 16)
            sp.wait_ge(same_stored, 16)
            for half in range(2):
                sp.dma_start(same1[half * FE:(half + 1) * FE, :],
                             same_dram[0:1, half * HALF:(half + 1) * HALF].to_broadcast([FE, HALF])
                             ).then_inc(same1_loaded, 16)

            p_v = p_tab.rearrange("(t p) f -> p t f", p=P)
            for q, g in enumerate(GROUPS):
                sp.wait_ge(p_relued, q + 1)
                sp.dma_start(p_v[:, g.start:g.stop, :], p_out[:, g.start:g.stop, :]).then_inc(p_stored, 16)

            sp.dma_start(mid_i[:, :], dst[0:1, HALF:HALF + 1].to_broadcast([P, 1])).then_inc(mid_loaded, 16)
            load_row(bias_g2[:, 0, :], b_gn, w12_loaded)
            load_row(bias_g2[:, 1, :], b_gin, w12_loaded)
            load_row(bias_12[:, 0, :], b1, w12_loaded)
            load_row(bias_12[:, 1, :], b2, w12_loaded)
            sp.dma_start(wgin[:, :], w_gin).then_inc(w12_loaded, 16)
            sp.dma_start(w1[:, :, :], w1_t.rearrange("(b p) f -> p b f", p=P)).then_inc(w12_loaded, 16)
            sp.dma_start(w2[:, :, :], w2_t.rearrange("(b p) f -> p b f", p=P)).then_inc(w12_loaded, 16)
            sp.dma_start(u0[:, :], u[0:1, :].rearrange("o f -> f o"), allow_slow_non_contiguous=True).then_inc(w12_loaded, 16)

            sp.wait_ge(consts, 1)
            for k in range(RING):
                zero1(0, k)
            with sp.Fori(1, NCH1 // RING) as i:
                for k in range(RING):
                    feed1(i, k)
                    zero1(i, k)

            sp.wait_ge(row_made, NCH1)
            sp.dma_start(same2[:, :], same_dram[0:1, :].to_broadcast([P, EPAD])).then_inc(same2_loaded, 16)
            for k in range(RING):
                sp.wait_ge(stored1[k], 16 * (NCH1 // RING))
            sp.dma_start(carry[:, :], max_rows[HALF - 1:HALF, 0:FE].to_broadcast([P, FE])).then_inc(carry_loaded, 16)

            b_v = b_tab.rearrange("(t p) f -> p t f", p=P)
            for q, g in enumerate(GROUPS):
                sp.wait_ge(b_ready, q + 1)
                sp.dma_start(b_v[:, g.start:g.stop, :], ab[:, g.start:g.stop, F:2 * F]).then_inc(b_stored, 16)

            seed_chunks = seed_rows.rearrange("(c p r) f -> c p (r f)", p=P, r=TPC)

            def feed2(i, k):
                c, k4 = RING2 * i + k, k % RING
                if not isinstance(i, int):
                    sp.wait_ge(got2[k], 16 * TPC * i)
                elif k < RING:
                    sp.wait_ge(got1[k], 16 * 2 * TPG * (NCH1 // RING))
                sp.dma_start(pick[:, k, 0:TPC], src2[bass.ds(c, 1), :, :].rearrange("o p c -> (o p) c")
                             ).then_inc(pick2_loaded[k], 16)
                if not isinstance(i, int) or k >= RING:
                    sp.wait_ge(summed, c - RING + 1)
                sp.dma_start(edges[:, k4, :], edge_t[bass.ds(c, 1), :, :].rearrange("o p c -> (o p) c")
                             ).then_inc(edges_loaded[k4], 16)
                if isinstance(i, int) and k == 0:
                    sp.wait_ge(seeded, 16 * NT)
                sp.dma_start(seeds[:, k4, :, :].rearrange("p r f -> p (r f)"),
                             seed_chunks[bass.ds(c, 1), :, :].rearrange("o p c -> (o p) c")
                             ).then_inc(seeds_loaded[k4], 16)

            for k in range(RING2):
                feed2(0, k)
            with sp.Fori(1, NCH // RING2) as i:
                for k in range(RING2):
                    feed2(i, k)

            for q, g in enumerate(GROUPS):
                sp.wait_ge(out_ready, q + 1)
                full = range(g.start, min(g.stop, N_NODES // P))
                if len(full):
                    sp.dma_start(out[full.start * P:full.stop * P, :].rearrange("(t p) f -> p t f", p=P),
                                 xs[:, full.start:full.stop, :]).then_inc(out_stored, 16)
            left = N_NODES % P
            sp.dma_start(out[N_NODES - left:, :], xs[0:left, NT - 1, :]).then_inc(out_stored, 16)
            sp.wait_ge(out_stored, 16 * (sum(g.start < N_NODES // P for g in GROUPS) + 1))

        @block.gpsimd
        def _(pool):
            nc.gpsimd.iota(iota_i[:, :], [[1, P]], base=0, channel_multiplier=0)
            nc.gpsimd.iota(node_i[:, :], [[P, NT]], base=0, channel_multiplier=1).then_inc(iota_ready, 1)
            nc.gpsimd.memset(ident[:, :], 1.0).then_inc(s_pool, 1)
            nc.gpsimd.memset(below[:, :], 1.0).then_inc(s_pool, 1)
            nc.gpsimd.memset(zeros[:, :], 0.0)
            nc.gpsimd.memset(zeros_bf[:, :], 0.0)
            pool.wait_ge(s_pool, 2)
            nc.gpsimd.affine_select(out=ident[:, :], in_=ident[:, :], compare_op=ALU.is_equal, fill=0.0,
                                    base=0, pattern=[[1, P]], channel_multiplier=-1).then_inc(s_pool, 1)
            nc.gpsimd.affine_select(out=below[:, :], in_=below[:, :], compare_op=ALU.is_gt, fill=0.0,
                                    base=0, pattern=[[1, P]], channel_multiplier=-1).then_inc(s_pool, 1)
            pool.wait_ge(s_pool, 4)
            nc.gpsimd.drain().then_inc(consts, 1)

            for q, g in enumerate(GROUPS):
                pool.wait_ge(norm_ready, q + 1)
                if q >= 2:
                    pool.wait_ge(ht_made, q - 1)
                for j, t in enumerate(g):
                    last = nc.gpsimd.tensor_scalar(h[:, q % 2, j, :], xs[:, t, :], rstd[:, t:t + 1], shift[:, t:t + 1],
                                                   ALU.mult, ALU.add)
                last.then_inc(h_ready, 1)

            pool.wait_ge(p_stored, 16 * NG)

            def gather1(i, k):
                g = RING * i + k
                pool.wait_ge(pick1_loaded[k], 16 * i + 16)
                if not isinstance(i, int):
                    pool.wait_ge(rows_t, g - RING + 1)
                pool.sem_inc(turn, 1)
                for j in range(TPG):
                    for half in range(2):
                        nc.gpsimd.indirect_dma_start(
                            out=rows[:, k, j, half * FE:(half + 1) * FE], out_offset=None, in_=p_tab[:, :],
                            in_offset=bass.IndirectOffsetOnAxis(ap=pick[:, k, 2 * j + half:2 * j + half + 1], axis=0),
                        ).then_inc(got1[k], 16)

            for k in range(RING):
                gather1(0, k)
            with pool.Fori(1, NCH1 // RING) as i:
                for k in range(RING):
                    gather1(i, k)

            pool.wait_ge(rows_known, 1)
            for k in range(RING):
                pool.wait_ge(stored1[k], 16 * (NCH1 // RING))
            for t in range(NT):
                nc.gpsimd.indirect_dma_start(
                    out=agg1[:, t, :], out_offset=None, in_=max_rows_half[:, :],
                    in_offset=bass.IndirectOffsetOnAxis(ap=max_at[:, t:t + 1], axis=0),
                ).then_inc(agg1_got[t // TG], 16)
            pool.wait_ge(zeroed, 16 * NCH1)
            for t in range(NT):
                pool.wait_ge(a_ready, t // TG + 1)
                nc.gpsimd.indirect_dma_start(
                    out=seed_rows[:, :], out_offset=bass.IndirectOffsetOnAxis(ap=seed_at[:, t:t + 1], axis=0),
                    in_=ab[:, t, 0:F], in_offset=None, bounds_check=EPAD - 1, oob_is_err=False,
                ).then_inc(seeded, 16)

            pool.wait_ge(b_stored, 16 * NG)

            pool.wait_ge(rows_t, NCH1)

            def gather2(i, k):
                c = RING2 * i + k
                pool.wait_ge(pick2_loaded[k], 16 * i + 16)
                if not isinstance(i, int):
                    pool.wait_ge(summed, c - RING2 + 1)
                pool.sem_inc(turn, 1)
                for j in range(TPC):
                    nc.gpsimd.indirect_dma_start(
                        out=rows[:, k, j, :], out_offset=None, in_=b_tab[:, :],
                        in_offset=bass.IndirectOffsetOnAxis(ap=pick[:, k, j:j + 1], axis=0),
                    ).then_inc(got2[k], 16)

            for k in range(RING2):
                gather2(0, k)
            with pool.Fori(1, NCH // RING2) as i:
                for k in range(RING2):
                    gather2(i, k)

            for k in range(RING):
                pool.wait_ge(stored2[k], 16 * (NCH // RING))
            pool.wait_ge(b_stored, 16 * NG)
            for t in range(NT):
                nc.gpsimd.indirect_dma_start(
                    out=agg2[:, t, 0:F], out_offset=None, in_=sum_rows[:, :],
                    in_offset=bass.IndirectOffsetOnAxis(ap=last_at[:, t:t + 1], axis=0),
                ).then_inc(agg2_got[t // TG], 16)

        @block.scalar
        def _(act):
            def norm_std(q, phase):
                n, g = phase * NG + q, GROUPS[q]
                act.wait_ge(var_done, n + 1)
                nc.scalar.activation(std[:, g.start:g.stop], mv[:, g.start:g.stop, 1], ACT.Sqrt,
                                     bias=eps[:, 0:1]).then_inc(std_done, 1)

            def relu_ht(q, phase):
                n, g = phase * NG + q, GROUPS[q]
                act.wait_ge(ht_made, n + 1)
                nc.scalar.activation(ht[:, g.start:g.stop, :].rearrange("p t f -> p (t f)"),
                                     bank[n % 2][:, 0:len(g) * P], ACT.Relu).then_inc(ht_ready, 1)

            act.wait_ge(dve_consts, 1)
            nc.scalar.activation(std[:, 0:1], eps[:, 0:1], ACT.Sqrt).then_inc(act_warm, 1)
            act.wait_ge(act_warm, 1)
            for q in range(AHEAD):
                norm_std(q, 0)
            for q in range(NG):
                relu_ht(q, 0)
                if q + AHEAD < NG:
                    norm_std(q + AHEAD, 0)

            act.wait_ge(node_m_ready, 1)
            nc.scalar.copy(node_wide[:, :, :], node_m[:, :].unsqueeze(2).to_broadcast([P, NT, P])
                           ).then_inc(node_wide_ready, 1)
            act.wait_ge(p_relued, NG)
            nc.scalar.copy(parts[:, :, 0:FE], p_out[:, :, :]).then_inc(hi_made, 1)
            act.wait_ge(rest_made, 1)
            nc.scalar.copy(parts[:, :, FE:2 * FE], rest[:, :, :]).then_inc(mid_made, 1)

            max_chunks = max_rows.rearrange("(g p r) f -> g p (r f)", p=P, r=TPC)

            def store1(i, k):
                g = RING * i + k
                act.wait_ge(back1, g + 1)
                if not (isinstance(i, int) and i == 0):
                    act.wait_ge(stored1[k], 16 * i)
                nc.scalar.copy(back[:, k, :], bank[2 + k % 2]).then_inc(copied1, 1)
                act.wait_ge(copied1, g + 1)
                act.dma_start(max_chunks[bass.ds(g, 1), :, :].rearrange("o p c -> (o p) c"), back[:, k, :]
                              ).then_inc(stored1[k], 16)

            def split_row(i, k):
                g = RING * i + k
                act.wait_ge(row_made, g + 1)
                if not (isinstance(i, int) and g < 2):
                    act.wait_ge(rows_t, g - 1)
                nc.scalar.copy(row_parts[:, k % 2, :, :, :],
                               row_ps.rearrange("p (h s f) -> p s h f", h=2, s=NSPLIT)).then_inc(row_split, 1)

            split_row(0, 0)
            for k in range(RING):
                split_row((k + 1) // RING, (k + 1) % RING)
                store1(0, k)
            with act.Fori(1, NCH1 // RING - 1) as i:
                for k in range(RING):
                    split_row(i + (k + 1) // RING, (k + 1) % RING)
                    store1(i, k)
            for k in range(RING):
                if k + 1 < RING:
                    split_row(NCH1 // RING - 1, k + 1)
                store1(NCH1 // RING - 1, k)

            def copy_agg1(q):
                m = len(GROUPS[q])
                act.wait_ge(agg1_turned, q + 1)
                if q >= 2:
                    act.wait_ge(gin_done, q - 1)
                nc.scalar.copy(agg1_t[:, q % 2, 0:m, :].rearrange("p t f -> p (t f)"), bank[2][0:FE, 0:m * P]
                               ).then_inc(agg1_t_ready, 1)

            for q in range(AHEAD):
                copy_agg1(q)
                norm_std(q, 1)
            for q, g in enumerate(GROUPS):
                relu_ht(q, 1)
                if q + AHEAD < NG:
                    copy_agg1(q + AHEAD)
                act.wait_ge(b_made, q + 1)
                nc.scalar.copy(ab[:, g.start:g.stop, F:2 * F],
                               bank[6][:, 0:len(g) * F].rearrange("p (t f) -> p t f", f=F)).then_inc(b_ready, 1)
                if q + AHEAD < NG:
                    norm_std(q + AHEAD, 1)

            sum_chunks = sum_rows.rearrange("(c p r) f -> c p (r f)", p=P, r=TPC)

            def relu2(i, k):
                c = RING2 * i + k
                act.wait_ge(pre_ready, c + 1)
                nc.scalar.activation(msg[:, k % 2, :], msg[:, k % 2, :], ACT.Relu).then_inc(relued, 1)

            def store2(i, k):
                c, k4 = RING2 * i + k, k % RING
                act.wait_ge(back2, c + 1)
                if not isinstance(i, int) or c >= RING:
                    act.wait_ge(stored2[k4], 32 * i + 16 * (k // RING))
                nc.scalar.copy(back[:, k4, :], bank[4 + k % 2]).then_inc(copied2, 1)
                act.wait_ge(copied2, c + 1)
                act.dma_start(sum_chunks[bass.ds(c, 1), :, :].rearrange("o p c -> (o p) c"), back[:, k4, :]
                              ).then_inc(stored2[k4], 16)

            for k in range(RING2):
                relu2(0, k)
                if k > 0:
                    store2(0, k - 1)
            with act.Fori(1, NCH // RING2) as i:
                for k in range(RING2):
                    relu2(i, k)
                    store2(i if k else i - 1, (k - 1) % RING2)
            store2(NCH // RING2 - 1, RING2 - 1)

            for q, g in enumerate(GROUPS):
                m = len(g)
                act.wait_ge(agg2_turned, q + 1)
                if q >= 2:
                    act.wait_ge(out_prod, q - 1)
                nc.scalar.copy(agg2_t[:, q % 2, 0:m, :].rearrange("p t f -> p (t f)"), bank[7][:, 0:m * P]
                               ).then_inc(agg2_t_ready, 1)

        @block.vector
        def _(dve):
            nc.vector.memset(fill[:, 1, CH - 1:CH], 0.0)
            nc.vector.memset(scan[:, 1, CH - 1:CH], 0.0)
            nc.vector.memset(eps[:, :], EPS).then_inc(dve_consts, 1)
            dve.wait_ge(iota_ready, 1)
            nc.vector.tensor_scalar(node_m[:, :], node_i[:, :], MID, None, ALU.subtract).then_inc(node_m_ready, 1)

            def norm_stats(q, phase):
                n, g = phase * NG + q, GROUPS[q]
                for t in g:
                    last = nc.vector.bn_stats(stats[:, t, :], xs[:, t, :])
                last.then_inc(stats_done, 1)
                dve.wait_ge(stats_done, n + 1)
                for t in g:
                    last = nc.vector.bn_aggr(mv[:, t, :], stats[:, t, :])
                last.then_inc(var_done, 1)

            def norm_scale(q, phase):
                n, g = phase * NG + q, GROUPS[q]
                g0, g1 = g.start, g.stop
                dve.wait_ge(std_done, n + 1)
                nc.vector.reciprocal(rstd[:, g0:g1], std[:, g0:g1]).then_inc(rstd_done, 1)
                dve.wait_ge(rstd_done, n + 1)
                nc.vector.scalar_tensor_tensor(out=shift[:, g0:g1], in0=mv[:, g0:g1, 0], scalar=-1.0,
                                               in1=rstd[:, g0:g1], op0=ALU.mult, op1=ALU.mult
                                               ).then_inc(norm_ready, 1)

            def make_p(q):
                g = GROUPS[q]
                m = len(g)
                dve.wait_ge(p_made, q + 1)
                nc.vector.tensor_tensor(p_out[:, g.start:g.stop, :],
                                        bank[2 + q % 2][:, 0:m * FE].rearrange("p (t f) -> p t f", f=FE),
                                        bias_p[:, :].unsqueeze(1).to_broadcast([P, m, FE]), ALU.add).then_inc(p_pre, 1)
                dve.wait_ge(p_pre, q + 1)
                nc.vector.tensor_scalar_max(p_out[:, g.start:g.stop, :], p_out[:, g.start:g.stop, :], 0.0
                                            ).then_inc(p_relued, 1)

            for q in range(AHEAD):
                dve.wait_ge(x_loaded[q], 16)
                norm_stats(q, 0)
            dve.wait_ge(dst_loaded, 32)
            nc.vector.tensor_tensor(same_row[:, :], dst_now[:, :], dst_before[:, :], ALU.is_equal).then_inc(same_made, 1)
            for q in range(NG):
                norm_scale(q, 0)
                if q + AHEAD < NG:
                    dve.wait_ge(x_loaded[q + AHEAD], 16)
                    norm_stats(q + AHEAD, 0)
                if q == 0:
                    dve.wait_ge(w0_loaded, 16 * 3)
                else:
                    make_p(q - 1)
            make_p(NG - 1)
            dve.wait_ge(consts, 1)
            nc.vector.tensor_copy(ident_bf[:, :], ident[:, :])
            nc.vector.tensor_copy(ident_h[:, :], ident[:, :]).then_inc(idents_ready, 1)

            def stage(i, k):
                g = RING * i + k
                if not (isinstance(i, int) and g < 2):
                    dve.wait_ge(spread, g - 1)
                nc.vector.tensor_scalar(src_m[:, k % 2, :], src_i[:, bass.ds(g, 1), :].rearrange("p o h -> p (o h)"),
                                        MID, None, ALU.subtract).then_inc(staged, 1)

            dve.wait_ge(src_loaded, 16)
            stage(0, 0)
            stage(0, 1)
            dve.wait_ge(hi_made, 1)
            nc.vector.tensor_tensor(rest[:, :, :], p_out[:, :, :], parts[:, :, 0:FE], ALU.subtract).then_inc(rest_made, 1)
            for q, g in enumerate(GROUPS):
                dve.wait_ge(g_made, q + 1)
                dve.wait_ge(h_ready, q + 1)
                nc.vector.tensor_tensor(xs[:, g.start:g.stop, :], xs[:, g.start:g.stop, :],
                                        bank[5 + q % 2][:, 0:len(g) * F].rearrange("p (t f) -> p t f", f=F), ALU.add
                                        ).then_inc(x0_added, 1)
            dve.wait_ge(mid_made, 1)
            nc.vector.tensor_tensor(parts[:, :, 2 * FE:], rest[:, :, :], parts[:, :, FE:2 * FE], ALU.subtract
                                    ).then_inc(parts_ready, 1)
            nc.vector.tensor_scalar(dst_hi_i[:, :], dst_now[:, :], 7, None, ALU.arith_shift_right)
            nc.vector.tensor_scalar(dst_lo_i[:, :], dst_now[:, :], P - 1, None, ALU.bitwise_and).then_inc(split_dst, 1)
            dve.wait_ge(split_dst, 1)
            nc.vector.tensor_copy(dst_hi[:, :], dst_hi_i[:, :])
            nc.vector.tensor_copy(dst_lo[:, :], dst_lo_i[:, :])
            dve.wait_ge(iota_ready, 1)
            nc.vector.tensor_copy(iota_bf[:, :], iota_i[:, :])
            nc.vector.tensor_copy(node_f[:, :], node_i[:, :])
            dve.wait_ge(mid_loaded, 16)
            nc.vector.tensor_copy(mid_f[:, :], mid_i[:, :]).then_inc(split_dst, 1)
            dve.wait_ge(split_dst, 2)
            nc.vector.tensor_scalar(is_mid[:, :], node_f[:, :], mid_f[:, 0:1], None, ALU.is_equal)
            dve.wait_ge(w12_loaded, 16 * 8)
            nc.vector.tensor_copy(u0_wide[:, :], u0[:, 0:1].to_broadcast([P, P])).then_inc(u0_ready, 1)
            nc.vector.tensor_tensor(bias_g[:, :], bias_g2[:, 0, :], bias_g2[:, 1, :], ALU.add).then_inc(bias_ready, 1)
            dve.wait_ge(bias_ready, 1)
            dve.wait_ge(x0_added, NG)
            nc.vector.tensor_tensor(xs[:, :, :], xs[:, :, :], bias_g[:, :].unsqueeze(1).to_broadcast([P, NT, F]),
                                    ALU.add).then_inc(bias_ready, 1)
            dve.wait_ge(bias_made, 1)
            nc.vector.tensor_tensor(bias_a[:, :], bias_ps[:, 0:F], bias_12[:, 0, :], ALU.add)
            nc.vector.tensor_tensor(bias_y[:, :], bias_ps[:, F:], bias_12[:, 1, :], ALU.add).then_inc(bias_ready, 1)

            def hots(i, k):
                g = RING * i + k
                dve.wait_ge(spread, g + 1)
                if not (isinstance(i, int) and g < 2):
                    dve.wait_ge(row_made, g - 1)
                nc.vector.tensor_tensor(hot_src[:, k % 2, :, :, :],
                                        src_ps[k % 2].unsqueeze(1).to_broadcast([P, NT, 2, P]),
                                        node_wide[:, :, :].unsqueeze(2).to_broadcast([P, NT, 2, P]), ALU.is_equal
                                        ).then_inc(hot_src_ready, 1)

            def scan1(i, k):
                g = RING * i + k
                peeled = isinstance(i, int) and i == 0
                if not peeled or k >= 2:
                    dve.wait_ge(hist_added, g - 1)
                nc.vector.tensor_tensor(hot_hi[:, k % 2, :, :],
                                        dst_hi[:, bass.ds(HC * g, HC)].unsqueeze(2).to_broadcast([P, HC, NT]),
                                        iota_bf[:, 0:NT].unsqueeze(1).to_broadcast([P, HC, NT]), ALU.is_equal)
                nc.vector.tensor_tensor(hot_lo[:, k % 2, :, :],
                                        dst_lo[:, bass.ds(HC * g, HC)].unsqueeze(2).to_broadcast([P, HC, P]),
                                        iota_bf[:, :].unsqueeze(1).to_broadcast([P, HC, P]), ALU.is_equal
                                        ).then_inc(hot_ready, 1)
                if not peeled or k > 0:
                    dve.wait_ge(scanned1, g)
                if not peeled or k >= 2:
                    dve.wait_ge(back1, g - 1)
                dve.wait_ge(rows_t, g + 1)
                nc.vector.tensor_tensor_scan(scan[:, k % 2, :], same1[:, bass.ds(CH * g, CH)], bank[k % 2],
                                             scan[:, (k + 1) % 2, CH - 1:CH], ALU.mult, ALU.max
                                             ).then_inc(scanned1, 1)

            dve.wait_ge(same1_loaded, 32)
            dve.wait_ge(node_wide_ready, 1)
            hots(0, 0)
            hots(0, 1)
            stage(0, 2)
            for k in range(RING):
                scan1(0, k)
                hots((k + 2) // RING, (k + 2) % RING)
                stage((k + 3) // RING, (k + 3) % RING)
            with dve.Fori(1, NCH1 // RING - 1) as i:
                for k in range(RING):
                    scan1(i, k)
                    hots(i + (k + 2) // RING, (k + 2) % RING)
                    stage(i + (k + 3) // RING, (k + 3) % RING)
            for k in range(RING):
                scan1(NCH1 // RING - 1, k)
                if k + 2 < RING:
                    hots(NCH1 // RING - 1, k + 2)
                if k + 3 < RING:
                    stage(NCH1 // RING - 1, k + 3)

            step = [0]

            def link(ins):
                step[0] += 1
                ins.then_inc(seg_step, 1)
                dve.wait_ge(seg_step, step[0])

            dve.wait_ge(hist_done, 1)
            link(nc.vector.tensor_copy(count[:, :], hist))
            link(nc.vector.tensor_tensor_scan(upto[:, :], zeros_bf[0:NT, :], count[:, :], 0.0, ALU.add, ALU.add))
            dve.wait_ge(before_made, 1)
            link(nc.vector.tensor_copy(before[:, :], before_ps))
            link(nc.vector.tensor_scalar(end_row[:, :], upto[:, :], before[:, 0:1], None, ALU.add))
            dve.wait_ge(seg_moved, 1)
            nc.vector.tensor_copy(seg_end[:, :], seg_ps[:, 0:NT])
            link(nc.vector.tensor_copy(seg_count[:, :], seg_ps[:, NT:]))
            nc.vector.tensor_scalar(empty[:, :], seg_count[:, :], 0.0, None, ALU.is_equal)
            nc.vector.tensor_scalar(filled[:, :], seg_count[:, :], 0.0, None, ALU.is_gt)
            link(nc.vector.tensor_scalar(last_f[:, :], seg_end[:, :], -1.0, 0.0, ALU.add, ALU.max))
            link(nc.vector.tensor_scalar(upper[:, :], last_f[:, :], float(HALF), float(1 - EPAD), ALU.is_ge, ALU.mult))
            link(nc.vector.scalar_tensor_tensor(out=max_at_f[:, :], in0=last_f[:, :], scalar=2.0, in1=upper[:, :],
                                                op0=ALU.mult, op1=ALU.add))
            nc.vector.tensor_copy(last_at[:, :], last_f[:, :])
            link(nc.vector.tensor_copy(max_at[:, :], max_at_f[:, :]))
            nc.vector.engine_nop().then_inc(rows_known, 1)
            link(nc.vector.tensor_tensor(seed_at_f[:, :], seg_end[:, :], seg_count[:, :], ALU.subtract))
            link(nc.vector.scalar_tensor_tensor(out=seed_at_f[:, :], in0=empty[:, :], scalar=float(SKIP),
                                                in1=seed_at_f[:, :], op0=ALU.mult, op1=ALU.add))
            link(nc.vector.tensor_copy(seed_at[:, :], seed_at_f[:, :]))
            dve.wait_ge(carry_loaded, 16)
            link(nc.vector.tensor_tensor(carried[:, :, :], carry[:, :].unsqueeze(1).to_broadcast([P, NT, FE]),
                                         is_mid[:, :].unsqueeze(2).to_broadcast([P, NT, FE]), ALU.mult))

            nstep = [0]

            def nlink(ins):
                nstep[0] += 1
                ins.then_inc(node_step, 1)
                dve.wait_ge(node_step, nstep[0])

            def clean_agg1(q):
                g0, g1 = GROUPS[q].start, GROUPS[q].stop
                dve.wait_ge(agg1_got[q], 16 * (g1 - g0))
                nlink(nc.vector.tensor_tensor(agg1[:, g0:g1, :], agg1[:, g0:g1, :],
                                              filled[:, g0:g1].unsqueeze(2).to_broadcast([P, g1 - g0, FE]), ALU.mult))
                nc.vector.tensor_tensor(agg1[:, g0:g1, :], agg1[:, g0:g1, :], carried[:, g0:g1, :], ALU.max
                                        ).then_inc(agg1_ready, 1)

            def add_gin(q):
                g0, g1 = GROUPS[q].start, GROUPS[q].stop
                dve.wait_ge(gin_done, q + 1)
                nc.vector.tensor_tensor(xs[:, g0:g1, :], xs[:, g0:g1, :],
                                        bank[3][:, 0:(g1 - g0) * F].rearrange("p (t f) -> p t f", f=F), ALU.add
                                        ).then_inc(x1_ready, 1)
                dve.wait_ge(x1_ready, q + 1)

            def norm(q):
                n = NG + q
                norm_scale(q, 1)
                dve.wait_ge(norm_ready, n + 1)
                dve.wait_ge(ht_made, n - 1)
                for j, t in enumerate(GROUPS[q]):
                    last = nc.vector.tensor_scalar(h[:, n % 2, j, :], xs[:, t, :], rstd[:, t:t + 1], shift[:, t:t + 1],
                                                   ALU.mult, ALU.add)
                last.then_inc(h_ready, 1)

            dve.wait_ge(bias_ready, 3)
            clean_agg1(0)
            for q in range(AHEAD):
                clean_agg1(q + 1)
                add_gin(q)
                norm_stats(q, 1)
                norm(q)
            for q in range(NG):
                g0, g1 = GROUPS[q].start, GROUPS[q].stop
                if q + AHEAD < NG:
                    add_gin(q + AHEAD)
                    norm_stats(q + AHEAD, 1)
                if q + AHEAD + 1 < NG:
                    clean_agg1(q + AHEAD + 1)
                dve.wait_ge(a_made, q + 1)
                nc.vector.tensor_tensor(ab[:, g0:g1, 0:F], bank[5][:, 0:(g1 - g0) * F].rearrange("p (t f) -> p t f", f=F),
                                        bias_a[:, :].unsqueeze(1).to_broadcast([P, g1 - g0, F]), ALU.add
                                        ).then_inc(a_ready, 1)
                if q + AHEAD < NG:
                    norm(q + AHEAD)

            def fill2(i, k):
                c = RING2 * i + k
                peeled = isinstance(i, int)
                dve.wait_ge(seeds_t, c + 1)
                if not peeled or k > 0:
                    dve.wait_ge(filled2, c)
                nc.vector.tensor_tensor_scan(fill[:, k % 2, :], same2[:, bass.ds(CH * c, CH)], bank[k % 2],
                                             fill[:, (k + 1) % 2, CH - 1:CH], ALU.mult, ALU.add
                                             ).then_inc(filled2, 1)

            def join2(i, k):
                c = RING2 * i + k
                peeled = isinstance(i, int)
                dve.wait_ge(summed, c + 1)
                dve.wait_ge(filled2, c + 1)
                if not peeled or k >= 2:
                    dve.wait_ge(scanned2, c - 1)
                nc.vector.tensor_tensor(msg[:, k % 2, :], fill[:, k % 2, :], bank[2 + k % 2], ALU.add
                                        ).then_inc(pre_ready, 1)

            def scan2(i, k):
                c = RING2 * i + k
                peeled = isinstance(i, int) and i == 0
                dve.wait_ge(relued, c + 1)
                if not peeled or k > 0:
                    dve.wait_ge(scanned2, c)
                if not peeled or k >= 2:
                    dve.wait_ge(back2, c - 1)
                nc.vector.tensor_tensor_scan(scan[:, k % 2, :], same2[:, bass.ds(CH * c, CH)], msg[:, k % 2, :],
                                             scan[:, (k + 1) % 2, CH - 1:CH], ALU.mult, ALU.add
                                             ).then_inc(scanned2, 1)

            dve.wait_ge(same2_loaded, 16)
            for k in range(RING2):
                fill2(0, k)
                if k > 0:
                    scan2(0, k - 1)
                join2(0, k)
            with dve.Fori(1, NCH // RING2) as i:
                for k in range(RING2):
                    fill2(i, k)
                    scan2(i if k else i - 1, (k - 1) % RING2)
                    join2(i, k)
            scan2(NCH // RING2 - 1, RING2 - 1)

            def clean_agg2(q):
                g0, g1 = GROUPS[q].start, GROUPS[q].stop
                dve.wait_ge(agg2_got[q], 16 * (g1 - g0))
                nc.vector.tensor_tensor(agg2[:, g0:g1, 0:F], agg2[:, g0:g1, 0:F],
                                        filled[:, g0:g1].unsqueeze(2).to_broadcast([P, g1 - g0, F]), ALU.mult
                                        ).then_inc(agg2_ready, 1)

            clean_agg2(0)
            for q in range(NG):
                g0, g1 = GROUPS[q].start, GROUPS[q].stop
                m = g1 - g0
                if q + 1 < NG:
                    clean_agg2(q + 1)
                dve.wait_ge(out_prod, q + 1)
                nc.vector.tensor_tensor(res[:, q % 2, 0:m, :],
                                        bank[q][:, 0:m * F].rearrange("p (t f) -> p t f", f=F),
                                        bias_y[:, :].unsqueeze(1).to_broadcast([P, m, F]), ALU.add).then_inc(out_pre, 1)
                dve.wait_ge(out_pre, q + 1)
                nc.vector.scalar_tensor_tensor(out=xs[:, g0:g1, :].rearrange("p t f -> p (t f)"),
                                               in0=res[:, q % 2, 0:m, :].rearrange("p t f -> p (t f)"), scalar=0.0,
                                               in1=xs[:, g0:g1, :].rearrange("p t f -> p (t f)"),
                                               op0=ALU.max, op1=ALU.add).then_inc(out_ready, 1)

        @block.tensor
        def _(pe):
            def turn_h(q, phase):
                n = phase * NG + q
                pe.wait_ge(h_ready, n + 1)
                if n >= 2:
                    pe.wait_ge(ht_ready, n - 1)
                for j in range(len(GROUPS[q])):
                    last = nc.tensor.transpose(bank[n % 2][:, j * P:(j + 1) * P], h[:, n % 2, j, :], ident[:, :])
                last.then_inc(ht_made, 1)

            def times(to, q, weights, made, stop=True):
                w = weights.shape[-1]
                for j, t in enumerate(GROUPS[q]):
                    last = nc.tensor.matmul(to[:, j * w:(j + 1) * w], ht[:, t, :], weights, start=True, stop=stop)
                last.then_inc(made, 1)

            pe.wait_ge(consts, 1)
            pe.wait_ge(w0_loaded, 16 * 3)
            turn_h(0, 0)
            for q in range(NG):
                if q + 1 < NG:
                    turn_h(q + 1, 0)
                pe.wait_ge(ht_ready, q + 1)
                if q >= 2:
                    pe.wait_ge(p_pre, q - 1)
                times(bank[2 + q % 2], q, w0[:, 0:FE], p_made)
            for q in range(NG):
                if q >= 2:
                    pe.wait_ge(x0_added, q - 1)
                times(bank[5 + q % 2], q, w0[:, FE:], g_made)
            pe.wait_ge(u0_ready, 1)
            pe.wait_ge(x0_added, NG)
            nc.tensor.matmul(bias_ps[:, 0:F], u0_wide[:, :], w1[:, 3, :], start=True, stop=True)
            nc.tensor.matmul(bias_ps[:, F:], u0_wide[:, :], w2[:, 2, :], start=True, stop=True).then_inc(bias_made, 1)

            nc.tensor.matmul(hist, zeros_bf[:, 0:NT], zeros_bf[:, :], start=True, stop=False)

            def spread_src(i, k):
                g = RING * i + k
                pe.wait_ge(staged, g + 1)
                if not (isinstance(i, int) and g < 2):
                    pe.wait_ge(hot_src_ready, g - 1)
                for half in range(2):
                    last = nc.tensor.transpose(src_ps[k % 2][:, half, :],
                                               src_m[:, k % 2, half:half + 1].to_broadcast([P, P]), ident_h[:, :])
                last.then_inc(spread, 1)

            def make_rows(i, k):
                g = RING * i + k
                pe.wait_ge(hot_src_ready, g + 1)
                if not (isinstance(i, int) and g < 1):
                    pe.wait_ge(row_split, g)
                for half in range(2):
                    for t in range(NT):
                        last = nc.tensor.matmul(row_ps[:, half * NSPLIT * FE:(half + 1) * NSPLIT * FE],
                                                hot_src[:, k % 2, t, half, :], parts[:, t, :],
                                                start=(t == 0), stop=(t == NT - 1))
                last.then_inc(row_made, 1)

            def turn1(i, k):
                g = RING * i + k
                peeled = isinstance(i, int) and i == 0
                pe.wait_ge(got1[k], 16 * 2 * TPG * (i + 1))
                if not peeled or k >= 2:
                    pe.wait_ge(scanned1, g - 1)
                for j in range(TPG):
                    nc.tensor.transpose(bank[k % 2][:, j * P:(j + 1) * P], rows[:, k, j, :], ident[:, :])
                pe.wait_ge(row_split, g + 1)
                for s in range(NSPLIT):
                    last = nc.tensor.matmul(bank[k % 2][:, TPG * P:], row_parts[:, k % 2, s, :, :].rearrange("p h f -> p (h f)"),
                                            ident_bf[:, :], start=(s == 0), stop=(s == NSPLIT - 1))
                last.then_inc(rows_t, 1)
                if not (isinstance(i, int) and g + 2 >= NCH1):
                    spread_src(i + (k + 2) // RING, (k + 2) % RING)
                pe.wait_ge(hot_ready, g + 1)
                for j in range(HC):
                    last = nc.tensor.matmul(hist, hot_hi[:, k % 2, j, :], hot_lo[:, k % 2, j, :], start=False,
                                            stop=False)
                last.then_inc(hist_added, 1)
                if not (isinstance(i, int) and g + 1 >= NCH1):
                    make_rows(i + (k + 1) // RING, (k + 1) % RING)
                pe.wait_ge(scanned1, g + 1)
                if not peeled or k >= 2:
                    pe.wait_ge(copied1, g - 1)
                for j in range(TPC):
                    last = nc.tensor.transpose(bank[2 + k % 2][:, j * P:(j + 1) * P], scan[:, k % 2, j::TPC],
                                               ident[:, :])
                last.then_inc(back1, 1)

            pe.wait_ge(idents_ready, 1)
            pe.wait_ge(x0_added, NG)
            spread_src(0, 0)
            spread_src(0, 1)
            pe.wait_ge(parts_ready, 1)
            pe.wait_ge(bias_ready, 3)
            make_rows(0, 0)
            for k in range(RING):
                turn1(0, k)
            with pe.Fori(1, NCH1 // RING - 1) as i:
                for k in range(RING):
                    turn1(i, k)
            for k in range(RING):
                turn1(NCH1 // RING - 1, k)
            nc.tensor.matmul(hist, zeros_bf[:, 0:NT], zeros_bf[:, :], start=False, stop=True).then_inc(hist_done, 1)

            pe.wait_ge(seg_step, 2)
            nc.tensor.matmul(before_ps, below[0:NT, 0:NT], upto[:, P - 1:P], start=True, stop=True).then_inc(before_made, 1)
            pe.wait_ge(seg_step, 4)
            nc.tensor.transpose(seg_ps[:, 0:NT], end_row[:, :], ident[0:NT, 0:NT])
            nc.tensor.transpose(seg_ps[:, NT:], count[:, :], ident[0:NT, 0:NT]).then_inc(seg_moved, 1)

            pe.wait_ge(copied1, NCH1)
            pe.wait_ge(bias_ready, 3)

            def turn_agg1(q):
                pe.wait_ge(agg1_ready, q + 1)
                if q > 0:
                    pe.wait_ge(agg1_t_ready, q)
                for j, t in enumerate(GROUPS[q]):
                    last = nc.tensor.transpose(bank[2][0:FE, j * P:(j + 1) * P], agg1[:, t, :], ident[:, :])
                last.then_inc(agg1_turned, 1)

            def gin(q):
                pe.wait_ge(agg1_t_ready, q + 1)
                if q > 0:
                    pe.wait_ge(x1_ready, q)
                for j in range(len(GROUPS[q])):
                    last = nc.tensor.matmul(bank[3][:, j * F:(j + 1) * F], agg1_t[:, q % 2, j, :], wgin[:, :],
                                            start=True, stop=True)
                last.then_inc(gin_done, 1)

            for q in range(AHEAD):
                turn_agg1(q)
                gin(q)
            for q in range(NG):
                turn_h(q, 1)
                if q + AHEAD < NG:
                    turn_agg1(q + AHEAD)
                pe.wait_ge(ht_ready, NG + q + 1)
                if q > 0:
                    pe.wait_ge(b_ready, q)
                times(bank[6], q, w1[:, 1, :], b_made)
                if q + AHEAD < NG:
                    gin(q + AHEAD)
                if q > 0:
                    pe.wait_ge(a_ready, q)
                times(bank[5], q, w1[:, 0, :], a_made)

            pe.wait_ge(x1_ready, NG)
            pe.wait_ge(ht_ready, 2 * NG)

            def front2(i, k):
                c, k4 = RING2 * i + k, k % RING
                peeled = isinstance(i, int)
                pe.wait_ge(seeds_loaded[k4], 32 * i + 16 * (k // RING) + 16)
                if not peeled or k >= 2:
                    pe.wait_ge(filled2, c - 1)
                for j in range(TPC):
                    last = nc.tensor.transpose(bank[k % 2][:, j::TPC], seeds[:, k4, j, :], ident[:, :])
                last.then_inc(seeds_t, 1)
                pe.wait_ge(edges_loaded[k4], 32 * i + 16 * (k // RING) + 16)
                if not peeled or k >= 2:
                    pe.wait_ge(pre_ready, c - 1)
                nc.tensor.matmul(bank[2 + k % 2], w1[:, 2, :], edges[:, k4, :], start=True, stop=False)
                pe.wait_ge(got2[k], 16 * TPC * (i + 1))
                for j in range(TPC):
                    last = nc.tensor.matmul(bank[2 + k % 2][:, j * P:(j + 1) * P], rows[:, k, j, :], ident[:, :],
                                            start=False, stop=(j == TPC - 1))
                last.then_inc(summed, 1)

            def back_2(i, k):
                c = RING2 * i + k
                peeled = isinstance(i, int) and i == 0
                pe.wait_ge(scanned2, c + 1)
                if not peeled or k >= 2:
                    pe.wait_ge(copied2, c - 1)
                for j in range(TPC):
                    last = nc.tensor.transpose(bank[4 + k % 2][:, j * P:(j + 1) * P], scan[:, k % 2, j::TPC],
                                               ident[:, :])
                last.then_inc(back2, 1)

            for k in range(RING2):
                front2(0, k)
                if k > 0:
                    back_2(0, k - 1)
            with pe.Fori(1, NCH // RING2) as i:
                for k in range(RING2):
                    front2(i, k)
                    back_2(i if k else i - 1, (k - 1) % RING2)
            back_2(NCH // RING2 - 1, RING2 - 1)

            pe.wait_ge(pre_ready, NCH)
            pe.wait_ge(copied2, NCH)
            for q in range(NG):
                for j, t in enumerate(GROUPS[q]):
                    nc.tensor.matmul(bank[q][:, j * F:(j + 1) * F], ht[:, t, :], w2[:, 0, :], start=(j == 0), stop=False)

            def turn_agg2(q):
                pe.wait_ge(agg2_ready, q + 1)
                if q > 0:
                    pe.wait_ge(agg2_t_ready, q)
                for j, t in enumerate(GROUPS[q]):
                    last = nc.tensor.transpose(bank[7][:, j * P:(j + 1) * P], agg2[:, t, 0:F], ident[:, :])
                last.then_inc(agg2_turned, 1)

            for q, g in enumerate(GROUPS):
                turn_agg2(q)
                pe.wait_ge(agg2_t_ready, q + 1)
                for j in range(len(g)):
                    last = nc.tensor.matmul(bank[q][:, j * F:(j + 1) * F], agg2_t[:, q % 2, j, :], w2[:, 1, :],
                                            start=False, stop=(j == len(g) - 1))
                last.then_inc(out_prod, 1)


def kernel(x, src, dst, edge_attr_128, L0_gnn_W_fs, L0_gnn_b_fs, L0_gnn_W_gn, L0_gnn_b_gn, L0_gnn_W_gin,
           L0_gnn_b_gin, L1_gnn_u, L1_gnn_W1, L1_gnn_b1, L1_gnn_W2, L1_gnn_b2):
    import numpy as np
    import concourse.bacc as bacc
    from concourse.bass_utils import run_bass_kernel_spmd

    x, src, dst, e = (np.asarray(a) for a in (x, src, dst, edge_attr_128))
    src_pad = np.concatenate([src, np.zeros(EPAD - N_EDGES, src.dtype)])
    e_pad = np.concatenate([e, np.zeros((EPAD - N_EDGES, F), e.dtype)])
    arrays = {
        "x": np.concatenate([x, np.zeros((NPAD - N_NODES, F), x.dtype)]),
        "src1": src_pad.reshape(2, NCH1, TPC, P).transpose(1, 3, 2, 0)[:, :, :TPG, :].reshape(NCH1, P, 2 * TPG),
        "src_hot": src_pad.reshape(2, NCH1, TPC, P)[:, :, TPG, :].transpose(2, 1, 0).reshape(P, 2 * NCH1),
        "src2": src_pad.reshape(NCH, TPC, P).transpose(0, 2, 1),
        "dst": np.concatenate([np.full(1, -1, dst.dtype), dst, np.full(EPAD - N_EDGES, DST_PAD, dst.dtype)])[None, :],
        "edge_t": e_pad.reshape(NCH, CH, F).transpose(0, 2, 1),
        "w_fs": L0_gnn_W_fs, "b_fs": L0_gnn_b_fs, "w_gn": L0_gnn_W_gn, "b_gn": L0_gnn_b_gn,
        "w_gin": L0_gnn_W_gin, "b_gin": L0_gnn_b_gin, "u": L1_gnn_u, "w1_t": np.asarray(L1_gnn_W1).T,
        "b1": L1_gnn_b1, "w2_t": np.asarray(L1_gnn_W2).T, "b2": L1_gnn_b2,
    }
    arrays = {"in_" + name: np.ascontiguousarray(a) for name, a in arrays.items()}
    nc = bacc.Bacc("TRN2", target_bir_lowering=False, num_devices=1)
    ins = [nc.dram_tensor(name, a.shape, mybir.dt.from_np(a.dtype), kind="ExternalInput").ap()
           for name, a in arrays.items()]
    out = nc.dram_tensor("out", (N_NODES, F), mybir.dt.float32, kind="ExternalOutput").ap()
    gnn_program(nc, *ins, out)
    r = run_bass_kernel_spmd(nc, [arrays], core_ids=[0])
    return r.results[0]["out"]
```

```python
import concourse.bass as bass
from concourse import mybir
from contextlib import ExitStack

N_NODES, N_EDGES, F, FE = 3125, 53125, 128, 64
P = 128
NT = -(-N_NODES // P)
NPAD = NT * P
TG = 4
GROUPS = [range(t, min(t + TG, NT)) for t in range(0, NT, TG)]
NG = len(GROUPS)
AHEAD = 2
LAG = 3
CH = 512
TPC = CH // P
RING = 4
RING2 = 8
NCH = -(-N_EDGES // (CH * RING2)) * RING2
EPAD = NCH * CH
HALF = EPAD // 2
NCH1 = NCH // 2
EC = EPAD // P
TPG = TPC - 1
NSPLIT = 3
QUARTERS = [range(NT * n // RING, NT * (n + 1) // RING) for n in range(RING)]
NHOT = NCH // RING - 1
HC = EC // NCH1
EPS = 1e-5
DST_PAD = NPAD
WARM_UP = (36, 24)
MID = 2048
SKIP = 1 << 17


def gnn_program(nc, x, src1, src_hot1, src2, src_hot2, dst, edge_t, w_fs, b_fs, w_gn, b_gn, w_gin, b_gin, u, w1_t, b1,
                w2_t, b2, out):
    fp32, bf16, i32, u8 = mybir.dt.float32, mybir.dt.bfloat16, mybir.dt.int32, mybir.dt.uint8
    fp16 = mybir.dt.float16
    ALU = mybir.AluOpType
    ACT = mybir.ActivationFunctionType

    with ExitStack() as ctx:
        def sb(name, shape, dt=fp32):
            return ctx.enter_context(nc.sbuf_tensor(name, shape, dt))

        def sem(name):
            return ctx.enter_context(nc.semaphore(name))

        def sems(name, n):
            return [sem(f"{name}{i}") for i in range(n)]

        p_tab = nc.dram_tensor("p_tab", (NPAD, FE), fp32).ap()
        b_tab = nc.dram_tensor("b_tab", (NPAD, F), fp32).ap()
        same_dram = nc.dram_tensor("same_dram", (1, EPAD), u8).ap()
        max_rows = nc.dram_tensor("max_rows", (HALF, 2 * FE), fp32).ap()
        seed_rows = nc.dram_tensor("seed_rows", (EPAD, F), fp32).ap()
        sum_rows = nc.dram_tensor("sum_rows", (EPAD, F), fp32).ap()

        ident = sb("ident", [P, P])
        below = sb("below", [P, P])
        iota_i = sb("iota_i", [P, P], i32)
        iota_bf = sb("iota_bf", [P, P, HC], bf16)
        node_i = sb("node_i", [P, NT], i32)
        node_f = sb("node_f", [P, NT])
        node_m = sb("node_m", [P, NT])
        ident_bf = sb("ident_bf", [P, P], bf16)
        ident_h = sb("ident_h", [P, P], fp16)
        zeros_bf = sb("zeros_bf", [P, P], bf16)
        eps = sb("eps", [P, 1])
        w0 = sb("w0", [P, FE + F])
        wgin = sb("wgin", [FE, F])
        w1 = sb("w1", [P, 4, F])
        w2 = sb("w2", [P, 3, F])
        u0 = sb("u0", [P, 1])
        u0_wide = sb("u0_wide", [P, P])
        bias_p = sb("bias_p", [P, FE])
        bias_g2 = sb("bias_g2", [P, 2, F])
        bias_g = sb("bias_g", [P, F])
        bias_12 = sb("bias_12", [P, 2, F])
        bias_a = sb("bias_a", [P, F])
        bias_y = sb("bias_y", [P, F])

        xs = sb("xs", [P, NT, F])
        ht = sb("ht", [P, NT, F])
        stats = sb("stats", [P, NT, 6])
        mv = sb("mv", [P, NT, 2])
        std = sb("std", [P, NT])
        rstd = sb("rstd", [P, NT])
        shift = sb("shift", [P, NT])
        h = sb("h", [P, 2, TG, F])
        agg2_t = sb("agg2_t", [P, 2, 2, TG, P])
        res = agg2_t[:, 1, :, :, :]
        node_wide = agg2_t[:, :, :, :, :].rearrange("p a k t e -> p (a k t e)").bitcast(fp16)[:, 0:NT * P]
        node_wide = node_wide.rearrange("p (t e) -> p t e", t=NT)
        agg2_t = agg2_t[:, 0, :, :, :]
        p_out = sb("p_out", [P, NT, FE])
        agg1 = p_out
        carry = sb("carry", [P, FE])
        carried = ht[:, :, 0:FE]
        agg1_t = sb("agg1_t", [FE, 2, TG, P])
        place = sb("place", [P, HALF], u8)
        same1 = place[:, :]
        ab = place[:, 0:4 * NT * 2 * F].bitcast(fp32).rearrange("p (t c) -> p t c", t=NT)
        agg2 = ab
        b_parts = place[:, 0:4 * NT * 2 * F].bitcast(bf16).rearrange("p (t c) -> p t c", t=NT)
        hot_src2 = p_out[:, :, :].rearrange("p t f -> p (t f)").bitcast(bf16).rearrange("p (t e) -> p t e", t=NT)

        dst_hi = sb("dst_hi", [P, EC], bf16)
        dst_lo = sb("dst_lo", [P, EC], bf16)
        same_row = sb("same_row", [P, EC], u8)
        same2 = sb("same2", [P, EPAD], u8)
        sizes = [2 * NT * NSPLIT * FE, 2 * 2 * NT * 2 * P, 4 * NT * FE]
        ends = [sum(sizes[:n + 1]) for n in range(len(sizes))]
        parts, hot_src, rest = (same2[:, e - n:e].bitcast(dt)
                                for e, n, dt in zip(ends, sizes, (bf16, bf16, fp32)))
        parts = parts.rearrange("p (t c) -> p t c", t=NT)
        hot_src = hot_src.rearrange("p (k t h e) -> p k t h e", k=2, t=NT, h=2)
        rest = rest.rearrange("p (t f) -> p t f", t=NT)
        src_i = sb("src_i", [P, NCH1, 2], i32)
        src_m = sb("src_m", [P, 2, 2], fp16)
        row_parts = sb("row_parts", [P, 2, NSPLIT, 2, FE], bf16)
        row_parts2 = row_parts[:, 0, :, :, :].rearrange("p s h f -> p s (h f)")
        src_i2 = sb("src_i2", [P, NHOT], i32)
        src_m2 = sb("src_m2", [P, 1], fp16)
        hot_lo = sb("hot_lo", [P, 2, P, HC], bf16)
        hot_hi = sb("hot_hi", [P, 2, NT, HC], bf16)
        count = sb("count", [NT, P])
        upto = sb("upto", [NT, P])
        end_row = sb("end_row", [NT, P])
        before = sb("before", [NT, 1])
        seg_end = sb("seg_end", [P, NT])
        seg_count = sb("seg_count", [P, NT])
        empty = sb("empty", [P, NT])
        filled = sb("filled", [P, NT])
        last_f = sb("last_f", [P, NT])
        upper = sb("upper", [P, NT])
        max_at_f = sb("max_at_f", [P, NT])
        seed_at_f = sb("seed_at_f", [P, NT])
        last_at = sb("last_at", [P, NT], i32)
        max_at = sb("max_at", [P, NT], i32)
        seed_at = sb("seed_at", [P, NT], i32)
        mid_i = sb("mid_i", [P, 1], i32)
        mid_f = sb("mid_f", [P, 1])
        is_mid = sb("is_mid", [P, NT])

        pick = sb("pick", [P, RING2, 2 * TPC], i32)
        rows = sb("rows", [P, RING2, TPC, F])
        edges = sb("edges", [P, RING, CH])
        dst_now, dst_before, dst_hi_i, dst_lo_i = (edges[:, k, 0:EC].bitcast(i32) for k in range(RING))
        seeds = sb("seeds", [P, RING, TPC, F])
        zeros = seeds[:, 0:2, :, :].rearrange("p k r f -> p (k r f)")
        fill = sb("fill", [P, 2, CH])
        msg = sb("msg", [P, 2, CH])
        scan = sb("scan", [P, 2, CH])
        back = sb("back", [P, RING, CH])

        ps = [ctx.enter_context(nc.psum_tensor(f"ps{i}", [P, 2 * CH], fp32)) for i in range(4)]
        bank = [ps[i // 2][:, (i % 2) * CH:(i % 2 + 1) * CH] for i in range(8)]
        hist = bank[4][0:NT, 0:P]
        seg_ps = bank[4][:, P:P + 2 * NT]
        before_ps = bank[4][0:NT, 2 * P:2 * P + 1]
        bias_ps = bank[5][:, 0:2 * F]
        src_ps2 = bank[6][:, 0:P // 2].bitcast(fp16)
        row_ps2 = bank[7][:, 0:NSPLIT * F]
        row_ps = bank[5][:, 0:2 * NSPLIT * FE]
        src_ps = [bank[6 + k][:, 0:P].bitcast(fp16).rearrange("p (h e) -> p h e", h=2) for k in range(2)]

        x_loaded = sems("x_loaded", NG)
        w0_loaded = sem("w0_loaded")
        w12_loaded = sem("w12_loaded")
        dst_loaded = sem("dst_loaded")
        mid_loaded = sem("mid_loaded")
        s_pool = sem("s_pool")
        consts = sem("consts")
        dve_consts = sem("dve_consts")
        iota_ready = sem("iota_ready")
        bias_made = sem("bias_made")
        bias_ready = sem("bias_ready")
        u0_ready = sem("u0_ready")
        p_made = sem("p_made")
        g_made = sem("g_made")
        p_pre = sem("p_pre")
        p_relued = sem("p_relued")
        x0_added = sem("x0_added")
        a_made = sem("a_made")
        b_made = sem("b_made")
        a_ready = sem("a_ready")
        b_ready = sem("b_ready")
        split_dst = sem("split_dst")
        same_made = sem("same_made")
        same_stored = sem("same_stored")
        same1_loaded = sem("same1_loaded")
        same2_loaded = sem("same2_loaded")
        stats_done = sem("stats_done")
        var_done = sem("var_done")
        std_done = sem("std_done")
        rstd_done = sem("rstd_done")
        norm_ready = sem("norm_ready")
        h_ready = sem("h_ready")
        ht_made = sem("ht_made")
        ht_ready = sem("ht_ready")
        p_stored = sem("p_stored")
        act_warm = sem("act_warm")
        node_m_ready = sem("node_m_ready")
        node_wide_ready = sem("node_wide_ready")
        idents_ready = sem("idents_ready")
        src_loaded = sem("src_loaded")
        hi_made = sem("hi_made")
        rest_made = sem("rest_made")
        mid_made = sem("mid_made")
        parts_ready = sem("parts_ready")
        staged = sem("staged")
        spread = sem("spread")
        hot_src_ready = sem("hot_src_ready")
        row_made = sem("row_made")
        row_split = sem("row_split")
        b_hi_made = sem("b_hi_made")
        b_rest_made = sem("b_rest_made")
        b_mid_made = sem("b_mid_made")
        b_parts_ready = sem("b_parts_ready")
        staged2 = sem("staged2")
        spread2 = sem("spread2")
        hot2_ready = sem("hot2_ready")
        quarter_done = sem("quarter_done")
        row2_split = sem("row2_split")
        zeroed = sem("zeroed")
        pick1_loaded = sems("pick1_loaded", RING)
        got1 = sems("got1_", RING)
        turn = sem("turn")
        rows_t = sem("rows_t")
        hot_ready = sem("hot_ready")
        hist_added = sem("hist_added")
        hist_done = sem("hist_done")
        scanned1 = sem("scanned1")
        back1 = sem("back1")
        copied1 = sem("copied1")
        stored1 = sems("stored1_", RING)
        seg_step = sem("seg_step")
        before_made = sem("before_made")
        seg_moved = sem("seg_moved")
        rows_known = sem("rows_known")
        carry_loaded = sem("carry_loaded")
        agg1_got = sems("agg1_got", NG)
        node_step = sem("node_step")
        agg1_ready = sem("agg1_ready")
        agg1_turned = sem("agg1_turned")
        agg1_t_ready = sem("agg1_t_ready")
        gin_done = sem("gin_done")
        x1_ready = sem("x1_ready")
        b_stored = sem("b_stored")
        seeded = sem("seeded")
        pick2_loaded = sems("pick2_loaded", RING2)
        got2 = sems("got2_", RING2)
        edges_loaded = sems("edges_loaded", RING)
        seeds_loaded = sems("seeds_loaded", RING)
        seeds_t = sem("seeds_t")
        filled2 = sem("filled2")
        summed = sem("summed")
        pre_ready = sem("pre_ready")
        relued = sem("relued")
        scanned2 = sem("scanned2")
        back2 = sem("back2")
        copied2 = sem("copied2")
        stored2 = sems("stored2_", RING)
        agg2_got = sems("agg2_got", NG)
        agg2_ready = sem("agg2_ready")
        agg2_turned = sem("agg2_turned")
        agg2_t_ready = sem("agg2_t_ready")
        out_prod = sem("out_prod")
        out_pre = sem("out_pre")
        out_ready = sem("out_ready")
        out_stored = sem("out_stored")

        max_rows_half = max_rows.rearrange("r (h f) -> (r h) f", h=2)
        block = ctx.enter_context(nc.Block())

        def gathers2(k):
            return (TPC - 1, int(k == 0)) if k % RING == 0 else (TPC, 0)

        @block.sync
        def _(sp):
            x_v = x.rearrange("(t p) f -> p t f", p=P)

            def load_row(to, row, done):
                sp.dma_start(to, row.unsqueeze(0).to_broadcast([P, to.shape[-1]])).then_inc(done, 16)

            for q, g in enumerate(GROUPS):
                sp.dma_start(xs[:, g.start:g.stop, :], x_v[:, g.start:g.stop, :]).then_inc(x_loaded[q], 16)
                if q == 0:
                    sp.dma_start(dst_now[:, :], dst[:, 1:EPAD + 1].rearrange("o (p c) -> (o p) c", p=P)
                                 ).then_inc(dst_loaded, 16)
                    sp.dma_start(dst_before[:, :], dst[:, 0:EPAD].rearrange("o (p c) -> (o p) c", p=P)
                                 ).then_inc(dst_loaded, 16)
                if q == 1:
                    sp.dma_start(w0[:, 0:FE], w_fs).then_inc(w0_loaded, 16)
                    load_row(bias_p[:, :], b_fs, w0_loaded)
                    sp.dma_start(w0[:, FE:], w_gn).then_inc(w0_loaded, 16)
            sp.dma_start(src_i[:, :, :].rearrange("p g h -> p (g h)"), src_hot1).then_inc(src_loaded, 16)
            sp.dma_start(src_i2[:, :], src_hot2).then_inc(src_loaded, 16)

            seed_blocks = seed_rows.rearrange("(g p r) f -> g p (r f)", p=P, r=2 * TPC)

            def feed1(i, k):
                g = RING * i + k
                if not isinstance(i, int):
                    sp.wait_ge(got1[k], 16 * 2 * TPG * i)
                sp.dma_start(pick[:, k, 0:2 * TPG], src1[bass.ds(g, 1), :, :].rearrange("o p c -> (o p) c")
                             ).then_inc(pick1_loaded[k], 16)

            def zero1(i, k):
                g = RING * i + k
                sp.dma_start(seed_blocks[bass.ds(g, 1), :, :].rearrange("o p c -> (o p) c"), zeros[:, :]
                             ).then_inc(zeroed, 16)

            for k in range(RING):
                feed1(0, k)

            sp.wait_ge(same_made, 1)
            sp.dma_start(same_dram.rearrange("o (p c) -> (o p) c", p=P), same_row[:, :]).then_inc(same_stored, 16)

            p_v = p_tab.rearrange("(t p) f -> p t f", p=P)
            for q, g in enumerate(GROUPS):
                sp.wait_ge(p_relued, q + 1)
                sp.dma_start(p_v[:, g.start:g.stop, :], p_out[:, g.start:g.stop, :]).then_inc(p_stored, 16)

            sp.dma_start(mid_i[:, :], dst[0:1, HALF:HALF + 1].to_broadcast([P, 1])).then_inc(mid_loaded, 16)
            load_row(bias_g2[:, 0, :], b_gn, w12_loaded)
            load_row(bias_g2[:, 1, :], b_gin, w12_loaded)
            load_row(bias_12[:, 0, :], b1, w12_loaded)
            load_row(bias_12[:, 1, :], b2, w12_loaded)
            sp.dma_start(wgin[:, :], w_gin).then_inc(w12_loaded, 16)
            sp.dma_start(w1[:, :, :], w1_t.rearrange("(b p) f -> p b f", p=P)).then_inc(w12_loaded, 16)
            sp.dma_start(w2[:, :, :], w2_t.rearrange("(b p) f -> p b f", p=P)).then_inc(w12_loaded, 16)
            sp.dma_start(u0[:, :], u[0:1, :].rearrange("o f -> f o"), allow_slow_non_contiguous=True
                         ).then_inc(w12_loaded, 16)

            sp.wait_ge(same_stored, 16)
            for half in range(2):
                sp.dma_start(same1[half * FE:(half + 1) * FE, :],
                             same_dram[0:1, half * HALF:(half + 1) * HALF].to_broadcast([FE, HALF])
                             ).then_inc(same1_loaded, 16)

            sp.wait_ge(consts, 1)
            for k in range(RING):
                zero1(0, k)
            with sp.Fori(1, NCH1 // RING) as i:
                for k in range(RING):
                    feed1(i, k)
                    zero1(i, k)

            for k in range(RING):
                sp.wait_ge(stored1[k], 16 * (NCH1 // RING))
            sp.dma_start(carry[:, :], max_rows[HALF - 1:HALF, 0:FE].to_broadcast([P, FE])).then_inc(carry_loaded, 16)

            b_v = b_tab.rearrange("(t p) f -> p t f", p=P)
            sp.wait_ge(row_made, NCH1)
            piece = EPAD // NG // P * P
            for q, g in enumerate(GROUPS):
                e0, e1 = q * piece, (q + 1) * piece if q + 1 < NG else EPAD
                sp.wait_ge(agg1_got[q], 16 * len(g))
                sp.dma_start(same2[:, e0:e1], same_dram[0:1, e0:e1].to_broadcast([P, e1 - e0])).then_inc(same2_loaded, 16)
                sp.wait_ge(b_ready, q + 1)
                sp.dma_start(b_v[:, g.start:g.stop, :], ab[:, g.start:g.stop, F:2 * F]).then_inc(b_stored, 16)

            seed_chunks = seed_rows.rearrange("(c p r) f -> c p (r f)", p=P, r=TPC)

            def pick2(i, k):
                c = RING2 * i + k
                if not isinstance(i, int):
                    each, more = gathers2(k)
                    sp.wait_ge(got2[k], 16 * (each * i + more))
                elif k < RING:
                    sp.wait_ge(got1[k], 16 * 2 * TPG * (NCH1 // RING))
                sp.dma_start(pick[:, k, 0:TPC], src2[bass.ds(c, 1), :, :].rearrange("o p c -> (o p) c")
                             ).then_inc(pick2_loaded[k], 16)

            def feed2(i, k):
                c, k4 = RING2 * i + k, k % RING
                if not isinstance(i, int):
                    pick2(i, k)
                if not isinstance(i, int) or k >= RING:
                    sp.wait_ge(summed, c - RING + 1)
                sp.dma_start(edges[:, k4, :], edge_t[bass.ds(c, 1), :, :].rearrange("o p c -> (o p) c")
                             ).then_inc(edges_loaded[k4], 16)
                if isinstance(i, int) and k == 0:
                    sp.wait_ge(seeded, 16 * NT)
                sp.dma_start(seeds[:, k4, :, :].rearrange("p r f -> p (r f)"),
                             seed_chunks[bass.ds(c, 1), :, :].rearrange("o p c -> (o p) c")
                             ).then_inc(seeds_loaded[k4], 16)

            for k in range(RING2):
                pick2(0, k)
            for k in range(RING2):
                feed2(0, k)
            with sp.Fori(1, NCH // RING2) as i:
                for k in range(RING2):
                    feed2(i, k)

            for q, g in enumerate(GROUPS):
                sp.wait_ge(out_ready, q + 1)
                full = range(g.start, min(g.stop, N_NODES // P))
                if len(full):
                    sp.dma_start(out[full.start * P:full.stop * P, :].rearrange("(t p) f -> p t f", p=P),
                                 xs[:, full.start:full.stop, :]).then_inc(out_stored, 16)
            left = N_NODES % P
            sp.dma_start(out[N_NODES - left:, :], xs[0:left, NT - 1, :]).then_inc(out_stored, 16)
            sp.wait_ge(out_stored, 16 * (sum(g.start < N_NODES // P for g in GROUPS) + 1))

        @block.gpsimd
        def _(pool):
            nc.gpsimd.iota(iota_i[:, :], [[1, P]], base=0, channel_multiplier=0)
            nc.gpsimd.iota(node_i[:, :], [[P, NT]], base=0, channel_multiplier=1).then_inc(iota_ready, 1)
            nc.gpsimd.memset(ident[:, :], 1.0).then_inc(s_pool, 1)
            nc.gpsimd.memset(below[:, :], 1.0).then_inc(s_pool, 1)
            nc.gpsimd.memset(zeros[:, :], 0.0)
            nc.gpsimd.memset(zeros_bf[:, :], 0.0)
            pool.wait_ge(s_pool, 2)
            nc.gpsimd.affine_select(out=ident[:, :], in_=ident[:, :], compare_op=ALU.is_equal, fill=0.0,
                                    base=0, pattern=[[1, P]], channel_multiplier=-1).then_inc(s_pool, 1)
            nc.gpsimd.affine_select(out=below[:, :], in_=below[:, :], compare_op=ALU.is_gt, fill=0.0,
                                    base=0, pattern=[[1, P]], channel_multiplier=-1).then_inc(s_pool, 1)
            pool.wait_ge(s_pool, 4)
            nc.gpsimd.drain().then_inc(consts, 1)

            for q, g in enumerate(GROUPS):
                pool.wait_ge(norm_ready, q + 1)
                if q >= 2:
                    pool.wait_ge(ht_made, q - 1)
                for j, t in enumerate(g):
                    last = nc.gpsimd.tensor_scalar(h[:, q % 2, j, :], xs[:, t, :], rstd[:, t:t + 1], shift[:, t:t + 1],
                                                   ALU.mult, ALU.add)
                last.then_inc(h_ready, 1)

            pool.wait_ge(p_stored, 16 * NG)

            def gather1(i, k):
                g = RING * i + k
                pool.wait_ge(pick1_loaded[k], 16 * i + 16)
                if not isinstance(i, int):
                    pool.wait_ge(rows_t, g - RING + 1)
                pool.sem_inc(turn, 1)
                for j in range(TPG):
                    for half in range(2):
                        nc.gpsimd.indirect_dma_start(
                            out=rows[:, k, j, half * FE:(half + 1) * FE], out_offset=None, in_=p_tab[:, :],
                            in_offset=bass.IndirectOffsetOnAxis(ap=pick[:, k, 2 * j + half:2 * j + half + 1], axis=0),
                        ).then_inc(got1[k], 16)

            for k in range(RING):
                gather1(0, k)
            with pool.Fori(1, NCH1 // RING) as i:
                for k in range(RING):
                    gather1(i, k)

            pool.wait_ge(rows_known, 1)
            for k in range(RING):
                pool.wait_ge(stored1[k], 16 * (NCH1 // RING))
            for t in range(NT):
                nc.gpsimd.indirect_dma_start(
                    out=agg1[:, t, :], out_offset=None, in_=max_rows_half[:, :],
                    in_offset=bass.IndirectOffsetOnAxis(ap=max_at[:, t:t + 1], axis=0),
                ).then_inc(agg1_got[t // TG], 16)
            pool.wait_ge(zeroed, 16 * NCH1)
            for t in range(NT):
                pool.wait_ge(a_ready, t // TG + 1)
                nc.gpsimd.indirect_dma_start(
                    out=seed_rows[:, :], out_offset=bass.IndirectOffsetOnAxis(ap=seed_at[:, t:t + 1], axis=0),
                    in_=ab[:, t, 0:F], in_offset=None, bounds_check=EPAD - 1, oob_is_err=False,
                ).then_inc(seeded, 16)

            pool.wait_ge(b_stored, 16 * NG)

            pool.wait_ge(rows_t, NCH1)

            def gather2(i, k):
                c = RING2 * i + k
                pool.wait_ge(pick2_loaded[k], 16 * i + 16)
                if not isinstance(i, int):
                    pool.wait_ge(summed, c - RING2 + 1)
                pool.sem_inc(turn, 1)
                each, more = gathers2(k)
                for j in range(each + more if isinstance(i, int) else each):
                    nc.gpsimd.indirect_dma_start(
                        out=rows[:, k, j, :], out_offset=None, in_=b_tab[:, :],
                        in_offset=bass.IndirectOffsetOnAxis(ap=pick[:, k, j:j + 1], axis=0),
                    ).then_inc(got2[k], 16)

            for k in range(RING2):
                gather2(0, k)
            with pool.Fori(1, NCH // RING2) as i:
                for k in range(RING2):
                    gather2(i, k)

            for k in range(RING):
                pool.wait_ge(stored2[k], 16 * (NCH // RING))
            pool.wait_ge(b_stored, 16 * NG)
            for t in range(NT):
                nc.gpsimd.indirect_dma_start(
                    out=agg2[:, t, 0:F], out_offset=None, in_=sum_rows[:, :],
                    in_offset=bass.IndirectOffsetOnAxis(ap=last_at[:, t:t + 1], axis=0),
                ).then_inc(agg2_got[t // TG], 16)

        @block.scalar
        def _(act):
            def norm_std(q, phase):
                n, g = phase * NG + q, GROUPS[q]
                act.wait_ge(var_done, n + 1)
                nc.scalar.activation(std[:, g.start:g.stop], mv[:, g.start:g.stop, 1], ACT.Sqrt,
                                     bias=eps[:, 0:1]).then_inc(std_done, 1)

            def relu_ht(q, phase):
                n, g = phase * NG + q, GROUPS[q]
                act.wait_ge(ht_made, n + 1)
                nc.scalar.activation(ht[:, g.start:g.stop, :].rearrange("p t f -> p (t f)"),
                                     bank[n % 2][:, 0:len(g) * P], ACT.Relu).then_inc(ht_ready, 1)

            act.wait_ge(dve_consts, 1)
            nc.scalar.activation(std[:, 0:1], eps[:, 0:1], ACT.Sqrt).then_inc(act_warm, 1)
            act.wait_ge(act_warm, 1)
            for q in range(AHEAD + 1):
                norm_std(q, 0)
            for q in range(NG):
                relu_ht(q, 0)
                if q + AHEAD + 1 < NG:
                    norm_std(q + AHEAD + 1, 0)

            act.wait_ge(node_m_ready, 1)
            nc.scalar.copy(node_wide[:, :, :], node_m[:, :].unsqueeze(2).to_broadcast([P, NT, P])
                           ).then_inc(node_wide_ready, 1)
            act.wait_ge(p_relued, NG)
            nc.scalar.copy(parts[:, :, 0:FE], p_out[:, :, :]).then_inc(hi_made, 1)
            act.wait_ge(rest_made, 1)
            nc.scalar.copy(parts[:, :, FE:2 * FE], rest[:, :, :]).then_inc(mid_made, 1)

            max_chunks = max_rows.rearrange("(g p r) f -> g p (r f)", p=P, r=TPC)

            def store1(i, k):
                g = RING * i + k
                act.wait_ge(back1, g + 1)
                if not (isinstance(i, int) and i == 0):
                    act.wait_ge(stored1[k], 16 * i)
                nc.scalar.copy(back[:, k, :], bank[2 + k % 2]).then_inc(copied1, 1)
                act.wait_ge(copied1, g + 1)
                act.dma_start(max_chunks[bass.ds(g, 1), :, :].rearrange("o p c -> (o p) c"), back[:, k, :]
                              ).then_inc(stored1[k], 16)

            def split_row(i, k):
                g = RING * i + k
                act.wait_ge(row_made, g + 1)
                if not (isinstance(i, int) and g < 2):
                    act.wait_ge(rows_t, g - 1)
                nc.scalar.copy(row_parts[:, k % 2, :, :, :],
                               row_ps.rearrange("p (h s f) -> p s h f", h=2, s=NSPLIT)).then_inc(row_split, 1)

            split_row(0, 0)
            for k in range(RING):
                split_row((k + 1) // RING, (k + 1) % RING)
                store1(0, k)
            with act.Fori(1, NCH1 // RING - 1) as i:
                for k in range(RING):
                    split_row(i + (k + 1) // RING, (k + 1) % RING)
                    store1(i, k)
            for k in range(RING):
                if k + 1 < RING:
                    split_row(NCH1 // RING - 1, k + 1)
                store1(NCH1 // RING - 1, k)

            def copy_agg1(q):
                m = len(GROUPS[q])
                act.wait_ge(agg1_turned, q + 1)
                if q >= 2:
                    act.wait_ge(gin_done, q - 1)
                nc.scalar.copy(agg1_t[:, q % 2, 0:m, :].rearrange("p t f -> p (t f)"), bank[2][0:FE, 0:m * P]
                               ).then_inc(agg1_t_ready, 1)

            for q in range(AHEAD):
                copy_agg1(q)
                norm_std(q, 1)
            for q, g in enumerate(GROUPS):
                relu_ht(q, 1)
                if q + AHEAD < NG:
                    copy_agg1(q + AHEAD)
                act.wait_ge(b_made, q + 1)
                nc.scalar.copy(ab[:, g.start:g.stop, F:2 * F],
                               bank[6][:, 0:len(g) * F].rearrange("p (t f) -> p t f", f=F)).then_inc(b_ready, 1)
                if q + AHEAD < NG:
                    norm_std(q + AHEAD, 1)

            sum_chunks = sum_rows.rearrange("(c p r) f -> c p (r f)", p=P, r=TPC)

            def relu2(i, k):
                c = RING2 * i + k
                act.wait_ge(pre_ready, c + 1)
                nc.scalar.activation(msg[:, k % 2, :], msg[:, k % 2, :], ACT.Relu).then_inc(relued, 1)

            def store2(i, k):
                c, k4 = RING2 * i + k, k % RING
                act.wait_ge(back2, c + 1)
                if not (isinstance(i, int) and c < RING):
                    act.wait_ge(stored2[k4], 32 * i + 16 * (k // RING))
                nc.scalar.copy(back[:, k4, :], bank[4 + k % 2]).then_inc(copied2, 1)
                act.wait_ge(copied2, c + 1)
                act.dma_start(sum_chunks[bass.ds(c, 1), :, :].rearrange("o p c -> (o p) c"), back[:, k4, :]
                              ).then_inc(stored2[k4], 16)

            def split_row2(i, k):
                pe_rows = 2 * i + k // RING
                act.wait_ge(quarter_done, RING * (pe_rows + 1))
                if not (isinstance(i, int) and i == 0):
                    act.wait_ge(summed, RING * pe_rows + 1)
                nc.scalar.copy(row_parts2.rearrange("p s f -> p (s f)"), row_ps2).then_inc(row2_split, 1)

            def finish2(i, k, last=False):
                if k % RING == RING - 1 and not (last and k >= RING):
                    split_row2(i, k)
                relu2(i, k)
                if not (isinstance(i, int) and i == 0 and k == 0):
                    store2(i if k else i - 1, (k - 1) % RING2)

            act.wait_ge(b_ready, NG)
            act.wait_ge(seeded, 16 * NT)
            for q, g in enumerate(GROUPS):
                nc.scalar.copy(b_parts[:, g.start:g.stop, 0:F], ab[:, g.start:g.stop, F:]).then_inc(b_hi_made, 1)
            for q, g in enumerate(GROUPS):
                act.wait_ge(b_rest_made, q + 1)
                nc.scalar.copy(b_parts[:, g.start:g.stop, F:2 * F], h[:, q % 2, 0:len(g), :]).then_inc(b_mid_made, 1)

            for k in range(RING2):
                finish2(0, k)
            with act.Fori(1, NCH // RING2 - 1) as i:
                for k in range(RING2):
                    finish2(i, k)
            for k in range(RING2):
                finish2(NCH // RING2 - 1, k, last=True)
            store2(NCH // RING2 - 1, RING2 - 1)

            for q, g in enumerate(GROUPS):
                m = len(g)
                act.wait_ge(agg2_turned, q + 1)
                if q >= 2:
                    act.wait_ge(out_prod, q - 1)
                nc.scalar.copy(agg2_t[:, q % 2, 0:m, :].rearrange("p t f -> p (t f)"), bank[7][:, 0:m * P]
                               ).then_inc(agg2_t_ready, 1)

        @block.vector
        def _(dve):
            nc.vector.memset(fill[:, 1, CH - 1:CH], 0.0)
            nc.vector.memset(scan[:, 1, CH - 1:CH], 0.0)
            nc.vector.memset(eps[:, :], EPS).then_inc(dve_consts, 1)
            dve.wait_ge(iota_ready, 1)
            nc.vector.tensor_scalar(node_m[:, :], node_i[:, :], MID, None, ALU.subtract).then_inc(node_m_ready, 1)

            def norm_stats(q, phase):
                n, g = phase * NG + q, GROUPS[q]
                for t in g:
                    last = nc.vector.bn_stats(stats[:, t, :], xs[:, t, :])
                last.then_inc(stats_done, 1)
                dve.wait_ge(stats_done, n + 1)
                for t in g:
                    last = nc.vector.bn_aggr(mv[:, t, :], stats[:, t, :])
                last.then_inc(var_done, 1)

            def norm_scale(q, phase):
                n, g = phase * NG + q, GROUPS[q]
                g0, g1 = g.start, g.stop
                dve.wait_ge(std_done, n + 1)
                nc.vector.reciprocal(rstd[:, g0:g1], std[:, g0:g1]).then_inc(rstd_done, 1)
                dve.wait_ge(rstd_done, n + 1)
                nc.vector.scalar_tensor_tensor(out=shift[:, g0:g1], in0=mv[:, g0:g1, 0], scalar=-1.0,
                                               in1=rstd[:, g0:g1], op0=ALU.mult, op1=ALU.mult
                                               ).then_inc(norm_ready, 1)

            def make_p(q):
                g = GROUPS[q]
                m = len(g)
                dve.wait_ge(p_made, q + 1)
                nc.vector.tensor_tensor(p_out[:, g.start:g.stop, :],
                                        bank[2 + q % LAG][:, 0:m * FE].rearrange("p (t f) -> p t f", f=FE),
                                        bias_p[:, :].unsqueeze(1).to_broadcast([P, m, FE]), ALU.add).then_inc(p_pre, 1)
                dve.wait_ge(p_pre, q + 1)
                nc.vector.tensor_scalar_max(p_out[:, g.start:g.stop, :], p_out[:, g.start:g.stop, :], 0.0
                                            ).then_inc(p_relued, 1)

            for q in range(AHEAD):
                dve.wait_ge(x_loaded[q], 16)
                norm_stats(q, 0)
                if q == 0:
                    norm_scale(0, 0)
            for q in range(NG):
                if q > 0:
                    norm_scale(q, 0)
                if q == 1:
                    dve.wait_ge(dst_loaded, 32)
                    nc.vector.tensor_tensor(same_row[:, :], dst_now[:, :], dst_before[:, :], ALU.is_equal
                                            ).then_inc(same_made, 1)
                if q + AHEAD < NG:
                    dve.wait_ge(x_loaded[q + AHEAD], 16)
                    norm_stats(q + AHEAD, 0)
                if q == LAG:
                    dve.wait_ge(w0_loaded, 16 * 3)
                if q >= LAG:
                    make_p(q - LAG)
            for q in range(NG - LAG, NG):
                make_p(q)
            dve.wait_ge(consts, 1)
            nc.vector.tensor_copy(ident_bf[:, :], ident[:, :])
            nc.vector.tensor_copy(ident_h[:, :], ident[:, :]).then_inc(idents_ready, 1)

            def stage(i, k):
                g = RING * i + k
                if not (isinstance(i, int) and g < 2):
                    dve.wait_ge(spread, g - 1)
                nc.vector.tensor_scalar(src_m[:, k % 2, :], src_i[:, bass.ds(g, 1), :].rearrange("p o h -> p (o h)"),
                                        MID, None, ALU.subtract).then_inc(staged, 1)

            def hots(i, k):
                g = RING * i + k
                dve.wait_ge(spread, g + 1)
                if not (isinstance(i, int) and g < 2):
                    dve.wait_ge(row_made, g - 1)
                nc.vector.tensor_tensor(hot_src[:, k % 2, :, :, :],
                                        src_ps[k % 2].unsqueeze(1).to_broadcast([P, NT, 2, P]),
                                        node_wide[:, :, :].unsqueeze(2).to_broadcast([P, NT, 2, P]), ALU.is_equal
                                        ).then_inc(hot_src_ready, 1)

            dve.wait_ge(src_loaded, 32)
            stage(0, 0)
            stage(0, 1)
            dve.wait_ge(node_wide_ready, 1)
            hots(0, 0)
            dve.wait_ge(hi_made, 1)
            nc.vector.tensor_tensor(rest[:, :, :], p_out[:, :, :], parts[:, :, 0:FE], ALU.subtract).then_inc(rest_made, 1)
            for q, g in enumerate(GROUPS):
                dve.wait_ge(g_made, q + 1)
                dve.wait_ge(h_ready, q + 1)
                nc.vector.tensor_tensor(xs[:, g.start:g.stop, :], xs[:, g.start:g.stop, :],
                                        bank[q % 2][:, 0:len(g) * F].rearrange("p (t f) -> p t f", f=F), ALU.add
                                        ).then_inc(x0_added, 1)
                if q == NG // 2:
                    dve.wait_ge(mid_made, 1)
                    nc.vector.tensor_tensor(parts[:, :, 2 * FE:], rest[:, :, :], parts[:, :, FE:2 * FE], ALU.subtract
                                            ).then_inc(parts_ready, 1)
            nc.vector.tensor_scalar(dst_hi_i[:, :], dst_now[:, :], 7, None, ALU.arith_shift_right)
            nc.vector.tensor_scalar(dst_lo_i[:, :], dst_now[:, :], P - 1, None, ALU.bitwise_and).then_inc(split_dst, 1)
            dve.wait_ge(split_dst, 1)
            nc.vector.tensor_copy(dst_hi[:, :], dst_hi_i[:, :])
            nc.vector.tensor_copy(dst_lo[:, :], dst_lo_i[:, :])
            dve.wait_ge(iota_ready, 1)
            nc.vector.tensor_copy(iota_bf[:, :, :], iota_i[:, :].unsqueeze(2).to_broadcast([P, P, HC]))
            nc.vector.tensor_copy(node_f[:, :], node_i[:, :])
            dve.wait_ge(mid_loaded, 16)
            nc.vector.tensor_copy(mid_f[:, :], mid_i[:, :]).then_inc(split_dst, 1)
            dve.wait_ge(split_dst, 2)
            nc.vector.tensor_scalar(is_mid[:, :], node_f[:, :], mid_f[:, 0:1], None, ALU.is_equal)
            dve.wait_ge(w12_loaded, 16 * 8)
            nc.vector.tensor_copy(u0_wide[:, :], u0[:, 0:1].to_broadcast([P, P])).then_inc(u0_ready, 1)
            nc.vector.tensor_tensor(bias_g[:, :], bias_g2[:, 0, :], bias_g2[:, 1, :], ALU.add).then_inc(bias_ready, 1)
            dve.wait_ge(bias_made, 1)
            nc.vector.tensor_tensor(bias_a[:, :], bias_ps[:, 0:F], bias_12[:, 0, :], ALU.add)
            nc.vector.tensor_tensor(bias_y[:, :], bias_ps[:, F:], bias_12[:, 1, :], ALU.add).then_inc(bias_ready, 1)

            def scan1(i, k):
                g = RING * i + k
                peeled = isinstance(i, int) and i == 0
                if not peeled or k >= 2:
                    dve.wait_ge(hist_added, g - 1)
                nc.vector.tensor_tensor(hot_hi[:, k % 2, :, :],
                                        dst_hi[:, bass.ds(HC * g, HC)].unsqueeze(1).to_broadcast([P, NT, HC]),
                                        iota_bf[:, 0:NT, :], ALU.is_equal)
                nc.vector.tensor_tensor(hot_lo[:, k % 2, :, :],
                                        dst_lo[:, bass.ds(HC * g, HC)].unsqueeze(1).to_broadcast([P, P, HC]),
                                        iota_bf[:, :, :], ALU.is_equal
                                        ).then_inc(hot_ready, 1)
                if not peeled or k > 0:
                    dve.wait_ge(scanned1, g)
                if not peeled or k >= 2:
                    dve.wait_ge(back1, g - 1)
                dve.wait_ge(rows_t, g + 1)
                nc.vector.tensor_tensor_scan(scan[:, k % 2, :], same1[:, bass.ds(CH * g, CH)], bank[k % 2],
                                             scan[:, (k + 1) % 2, CH - 1:CH], ALU.mult, ALU.max
                                             ).then_inc(scanned1, 1)

            dve.wait_ge(same1_loaded, 32)
            hots(0, 1)
            stage(0, 2)
            for k in range(RING):
                scan1(0, k)
                hots((k + 2) // RING, (k + 2) % RING)
                stage((k + 3) // RING, (k + 3) % RING)
            with dve.Fori(1, NCH1 // RING - 1) as i:
                for k in range(RING):
                    scan1(i, k)
                    hots(i + (k + 2) // RING, (k + 2) % RING)
                    stage(i + (k + 3) // RING, (k + 3) % RING)
            for k in range(RING):
                scan1(NCH1 // RING - 1, k)
                if k + 2 < RING:
                    hots(NCH1 // RING - 1, k + 2)
                if k + 3 < RING:
                    stage(NCH1 // RING - 1, k + 3)

            step = [0]

            def link(ins):
                step[0] += 1
                ins.then_inc(seg_step, 1)
                dve.wait_ge(seg_step, step[0])

            dve.wait_ge(hist_done, 1)
            link(nc.vector.tensor_copy(count[:, :], hist))
            link(nc.vector.tensor_tensor_scan(upto[:, :], zeros_bf[0:NT, :], count[:, :], 0.0, ALU.add, ALU.add))
            dve.wait_ge(before_made, 1)
            link(nc.vector.tensor_copy(before[:, :], before_ps))
            link(nc.vector.tensor_scalar(end_row[:, :], upto[:, :], before[:, 0:1], None, ALU.add))
            dve.wait_ge(seg_moved, 1)
            nc.vector.tensor_copy(seg_end[:, :], seg_ps[:, 0:NT])
            link(nc.vector.tensor_copy(seg_count[:, :], seg_ps[:, NT:]))
            nc.vector.tensor_scalar(empty[:, :], seg_count[:, :], 0.0, None, ALU.is_equal)
            nc.vector.tensor_scalar(filled[:, :], seg_count[:, :], 0.0, None, ALU.is_gt)
            link(nc.vector.tensor_scalar(last_f[:, :], seg_end[:, :], -1.0, 0.0, ALU.add, ALU.max))
            link(nc.vector.tensor_scalar(upper[:, :], last_f[:, :], float(HALF), float(1 - EPAD), ALU.is_ge, ALU.mult))
            link(nc.vector.scalar_tensor_tensor(out=max_at_f[:, :], in0=last_f[:, :], scalar=2.0, in1=upper[:, :],
                                                op0=ALU.mult, op1=ALU.add))
            nc.vector.tensor_copy(last_at[:, :], last_f[:, :])
            link(nc.vector.tensor_copy(max_at[:, :], max_at_f[:, :]))
            nc.vector.engine_nop().then_inc(rows_known, 1)
            link(nc.vector.tensor_tensor(seed_at_f[:, :], seg_end[:, :], seg_count[:, :], ALU.subtract))
            link(nc.vector.scalar_tensor_tensor(out=seed_at_f[:, :], in0=empty[:, :], scalar=float(SKIP),
                                                in1=seed_at_f[:, :], op0=ALU.mult, op1=ALU.add))
            link(nc.vector.tensor_copy(seed_at[:, :], seed_at_f[:, :]))
            dve.wait_ge(carry_loaded, 16)
            link(nc.vector.tensor_tensor(carried[:, :, :], carry[:, :].unsqueeze(1).to_broadcast([P, NT, FE]),
                                         is_mid[:, :].unsqueeze(2).to_broadcast([P, NT, FE]), ALU.mult))

            dve.wait_ge(bias_ready, 2)
            dve.wait_ge(x0_added, NG)
            nc.vector.tensor_tensor(xs[:, :, :], xs[:, :, :], bias_g[:, :].unsqueeze(1).to_broadcast([P, NT, F]),
                                    ALU.add).then_inc(bias_ready, 1)

            nstep = [0]

            def nlink(ins):
                nstep[0] += 1
                ins.then_inc(node_step, 1)
                dve.wait_ge(node_step, nstep[0])

            def clean_agg1(q):
                g0, g1 = GROUPS[q].start, GROUPS[q].stop
                dve.wait_ge(agg1_got[q], 16 * (g1 - g0))
                nlink(nc.vector.tensor_tensor(agg1[:, g0:g1, :], agg1[:, g0:g1, :],
                                              filled[:, g0:g1].unsqueeze(2).to_broadcast([P, g1 - g0, FE]), ALU.mult))
                nc.vector.tensor_tensor(agg1[:, g0:g1, :], agg1[:, g0:g1, :], carried[:, g0:g1, :], ALU.max
                                        ).then_inc(agg1_ready, 1)

            def add_gin(q):
                g0, g1 = GROUPS[q].start, GROUPS[q].stop
                dve.wait_ge(gin_done, q + 1)
                nc.vector.tensor_tensor(xs[:, g0:g1, :], xs[:, g0:g1, :],
                                        bank[3][:, 0:(g1 - g0) * F].rearrange("p (t f) -> p t f", f=F), ALU.add
                                        ).then_inc(x1_ready, 1)
                dve.wait_ge(x1_ready, q + 1)

            def norm(q):
                n = NG + q
                norm_scale(q, 1)
                dve.wait_ge(norm_ready, n + 1)
                dve.wait_ge(ht_made, n - 1)
                for j, t in enumerate(GROUPS[q]):
                    last = nc.vector.tensor_scalar(h[:, n % 2, j, :], xs[:, t, :], rstd[:, t:t + 1], shift[:, t:t + 1],
                                                   ALU.mult, ALU.add)
                last.then_inc(h_ready, 1)

            dve.wait_ge(bias_ready, 3)
            clean_agg1(0)
            for q in range(AHEAD):
                clean_agg1(q + 1)
                add_gin(q)
                norm_stats(q, 1)
                norm(q)
            for q in range(NG):
                g0, g1 = GROUPS[q].start, GROUPS[q].stop
                if q + AHEAD < NG:
                    add_gin(q + AHEAD)
                    norm_stats(q + AHEAD, 1)
                if q + AHEAD + 1 < NG:
                    clean_agg1(q + AHEAD + 1)
                dve.wait_ge(a_made, q + 1)
                nc.vector.tensor_tensor(ab[:, g0:g1, 0:F], bank[5][:, 0:(g1 - g0) * F].rearrange("p (t f) -> p t f", f=F),
                                        bias_a[:, :].unsqueeze(1).to_broadcast([P, g1 - g0, F]), ALU.add
                                        ).then_inc(a_ready, 1)
                if q + AHEAD < NG:
                    norm(q + AHEAD)

            def fill2(i, k):
                c = RING2 * i + k
                peeled = isinstance(i, int) and i == 0
                dve.wait_ge(seeds_t, c + 1)
                if not peeled or k > 0:
                    dve.wait_ge(filled2, c)
                nc.vector.tensor_tensor_scan(fill[:, k % 2, :], same2[:, bass.ds(CH * c, CH)], bank[k % 2],
                                             fill[:, (k + 1) % 2, CH - 1:CH], ALU.mult, ALU.add
                                             ).then_inc(filled2, 1)

            def join2(i, k):
                c = RING2 * i + k
                peeled = isinstance(i, int) and i == 0
                dve.wait_ge(summed, c + 1)
                dve.wait_ge(filled2, c + 1)
                if not peeled or k >= 2:
                    dve.wait_ge(scanned2, c - 1)
                nc.vector.tensor_tensor(msg[:, k % 2, :], fill[:, k % 2, :], bank[2 + k % 2], ALU.add
                                        ).then_inc(pre_ready, 1)

            def scan2(i, k):
                c = RING2 * i + k
                peeled = isinstance(i, int) and i == 0
                dve.wait_ge(relued, c + 1)
                if not peeled or k > 0:
                    dve.wait_ge(scanned2, c)
                if not peeled or k >= 2:
                    dve.wait_ge(back2, c - 1)
                nc.vector.tensor_tensor_scan(scan[:, k % 2, :], same2[:, bass.ds(CH * c, CH)], msg[:, k % 2, :],
                                             scan[:, (k + 1) % 2, CH - 1:CH], ALU.mult, ALU.add
                                             ).then_inc(scanned2, 1)

            def stage2(n):
                if not (isinstance(n, int) and n == 0):
                    dve.wait_ge(spread2, n)
                nc.vector.tensor_scalar(src_m2[:, :], src_i2[:, bass.ds(n, 1)], MID, None, ALU.subtract
                                        ).then_inc(staged2, 1)

            def hots2(i, k):
                c, g = RING2 * i + k, QUARTERS[k % RING]
                dve.wait_ge(spread2, 2 * i + k // RING + 1)
                if not (isinstance(i, int) and c < RING):
                    dve.wait_ge(quarter_done, c - RING + 1)
                nc.vector.tensor_tensor(hot_src2[:, g.start:g.stop, :],
                                        src_ps2.unsqueeze(1).to_broadcast([P, len(g), P]),
                                        node_wide[:, g.start:g.stop, :], ALU.is_equal).then_inc(hot2_ready, 1)

            def work2(i, k, last=False):
                fill2(i, k)
                if not (isinstance(i, int) and i == 0 and k == 0):
                    scan2(i if k else i - 1, (k - 1) % RING2)
                join2(i, k)
                if not (last and k + 2 >= RING):
                    hots2(i + (k + 2) // RING2, (k + 2) % RING2)
                if k % RING == 0 and not last:
                    stage2(2 * i + k // RING + 1)

            stage2(0)
            for q in range(NG + 1):
                if q < NG:
                    g0, g1 = GROUPS[q].start, GROUPS[q].stop
                    dve.wait_ge(b_hi_made, q + 1)
                    if q >= 2:
                        dve.wait_ge(b_parts_ready, q - 1)
                    nc.vector.tensor_tensor(h[:, q % 2, 0:g1 - g0, :], ab[:, g0:g1, F:], b_parts[:, g0:g1, 0:F],
                                            ALU.subtract).then_inc(b_rest_made, 1)
                if q == 0:
                    dve.wait_ge(b_stored, 16 * NG)
                if q > 0:
                    g0, g1 = GROUPS[q - 1].start, GROUPS[q - 1].stop
                    dve.wait_ge(b_mid_made, q)
                    dve.wait_ge(b_rest_made, min(q + 1, NG))
                    nc.vector.tensor_tensor(b_parts[:, g0:g1, 2 * F:3 * F], h[:, (q - 1) % 2, 0:g1 - g0, :],
                                            b_parts[:, g0:g1, F:2 * F], ALU.subtract).then_inc(b_parts_ready, 1)
            hots2(0, 0)
            hots2(0, 1)

            dve.wait_ge(same2_loaded, 16 * NG)
            for k in range(RING2):
                work2(0, k)
            with dve.Fori(1, NCH // RING2 - 1) as i:
                for k in range(RING2):
                    work2(i, k)
            for k in range(RING2):
                work2(NCH // RING2 - 1, k, last=True)
            scan2(NCH // RING2 - 1, RING2 - 1)

            def clean_agg2(q):
                g0, g1 = GROUPS[q].start, GROUPS[q].stop
                dve.wait_ge(agg2_got[q], 16 * (g1 - g0))
                nc.vector.tensor_tensor(agg2[:, g0:g1, 0:F], agg2[:, g0:g1, 0:F],
                                        filled[:, g0:g1].unsqueeze(2).to_broadcast([P, g1 - g0, F]), ALU.mult
                                        ).then_inc(agg2_ready, 1)

            clean_agg2(0)
            for q in range(NG):
                g0, g1 = GROUPS[q].start, GROUPS[q].stop
                m = g1 - g0
                if q + 1 < NG:
                    clean_agg2(q + 1)
                dve.wait_ge(out_prod, q + 1)
                nc.vector.tensor_tensor(res[:, q % 2, 0:m, :],
                                        bank[q][:, 0:m * F].rearrange("p (t f) -> p t f", f=F),
                                        bias_y[:, :].unsqueeze(1).to_broadcast([P, m, F]), ALU.add).then_inc(out_pre, 1)
                dve.wait_ge(out_pre, q + 1)
                nc.vector.scalar_tensor_tensor(out=xs[:, g0:g1, :].rearrange("p t f -> p (t f)"),
                                               in0=res[:, q % 2, 0:m, :].rearrange("p t f -> p (t f)"), scalar=0.0,
                                               in1=xs[:, g0:g1, :].rearrange("p t f -> p (t f)"),
                                               op0=ALU.max, op1=ALU.add).then_inc(out_ready, 1)

        @block.tensor
        def _(pe):
            def turn_h(q, phase):
                n = phase * NG + q
                pe.wait_ge(h_ready, n + 1)
                if n >= 2:
                    pe.wait_ge(ht_ready, n - 1)
                for j in range(len(GROUPS[q])):
                    last = nc.tensor.transpose(bank[n % 2][:, j * P:(j + 1) * P], h[:, n % 2, j, :], ident[:, :])
                last.then_inc(ht_made, 1)

            def times(to, q, weights, made, stop=True):
                w = weights.shape[-1]
                for j, t in enumerate(GROUPS[q]):
                    last = nc.tensor.matmul(to[:, j * w:(j + 1) * w], ht[:, t, :], weights, start=True, stop=stop)
                last.then_inc(made, 1)

            def warm_up(n):
                for _ in range(n):
                    nc.tensor.matmul(bank[7][:, 0:P], zeros_bf[:, :], zeros_bf[:, :], start=True, stop=True)

            pe.wait_ge(consts, 1)
            warm_up(WARM_UP[0])
            pe.wait_ge(w0_loaded, 16 * 3)
            turn_h(0, 0)
            warm_up(WARM_UP[1])
            for q in range(NG):
                if q + 1 < NG:
                    turn_h(q + 1, 0)
                pe.wait_ge(ht_ready, q + 1)
                if q >= LAG:
                    pe.wait_ge(p_pre, q - LAG + 1)
                times(bank[2 + q % LAG], q, w0[:, 0:FE], p_made)
            def spread_src(i, k):
                g = RING * i + k
                pe.wait_ge(staged, g + 1)
                if not (isinstance(i, int) and g < 2):
                    pe.wait_ge(hot_src_ready, g - 1)
                for half in range(2):
                    last = nc.tensor.transpose(src_ps[k % 2][:, half, :],
                                               src_m[:, k % 2, half:half + 1].to_broadcast([P, P]), ident_h[:, :])
                last.then_inc(spread, 1)

            pe.wait_ge(idents_ready, 1)
            spread_src(0, 0)
            spread_src(0, 1)
            for q in range(NG):
                if q >= 2:
                    pe.wait_ge(x0_added, q - 1)
                times(bank[q % 2], q, w0[:, FE:], g_made)
            pe.wait_ge(u0_ready, 1)
            nc.tensor.matmul(bias_ps[:, 0:F], u0_wide[:, :], w1[:, 3, :], start=True, stop=True)
            nc.tensor.matmul(bias_ps[:, F:], u0_wide[:, :], w2[:, 2, :], start=True, stop=True).then_inc(bias_made, 1)

            nc.tensor.matmul(hist, zeros_bf[:, 0:NT], zeros_bf[:, :], start=True, stop=False)

            def make_rows(i, k):
                g = RING * i + k
                pe.wait_ge(hot_src_ready, g + 1)
                if not (isinstance(i, int) and g < 1):
                    pe.wait_ge(row_split, g)
                for half in range(2):
                    for t in range(NT):
                        last = nc.tensor.matmul(row_ps[:, half * NSPLIT * FE:(half + 1) * NSPLIT * FE],
                                                hot_src[:, k % 2, t, half, :], parts[:, t, :],
                                                start=(t == 0), stop=(t == NT - 1))
                last.then_inc(row_made, 1)

            def turn1(i, k):
                g = RING * i + k
                peeled = isinstance(i, int) and i == 0
                pe.wait_ge(got1[k], 16 * 2 * TPG * (i + 1))
                if not peeled or k >= 2:
                    pe.wait_ge(scanned1, g - 1)
                for j in range(TPG):
                    nc.tensor.transpose(bank[k % 2][:, j * P:(j + 1) * P], rows[:, k, j, :], ident[:, :])
                pe.wait_ge(row_split, g + 1)
                for part in range(NSPLIT):
                    last = nc.tensor.matmul(bank[k % 2][:, TPG * P:],
                                            row_parts[:, k % 2, part, :, :].rearrange("p h f -> p (h f)"),
                                            ident_bf[:, :], start=(part == 0), stop=(part == NSPLIT - 1))
                last.then_inc(rows_t, 1)
                if not (isinstance(i, int) and g + 2 >= NCH1):
                    spread_src(i + (k + 2) // RING, (k + 2) % RING)
                pe.wait_ge(hot_ready, g + 1)
                for j in range(HC):
                    last = nc.tensor.matmul(hist, hot_hi[:, k % 2, :, j], hot_lo[:, k % 2, :, j], start=False,
                                            stop=False)
                last.then_inc(hist_added, 1)
                if not (isinstance(i, int) and g + 1 >= NCH1):
                    make_rows(i + (k + 1) // RING, (k + 1) % RING)
                pe.wait_ge(scanned1, g + 1)
                if not peeled or k >= 2:
                    pe.wait_ge(copied1, g - 1)
                for j in range(TPC):
                    last = nc.tensor.transpose(bank[2 + k % 2][:, j * P:(j + 1) * P], scan[:, k % 2, j::TPC],
                                               ident[:, :])
                last.then_inc(back1, 1)

            pe.wait_ge(x0_added, NG)
            pe.wait_ge(parts_ready, 1)
            pe.wait_ge(bias_ready, 2)
            make_rows(0, 0)
            for k in range(RING):
                turn1(0, k)
            with pe.Fori(1, NCH1 // RING - 1) as i:
                for k in range(RING):
                    turn1(i, k)
            for k in range(RING):
                turn1(NCH1 // RING - 1, k)
            nc.tensor.matmul(hist, zeros_bf[:, 0:NT], zeros_bf[:, :], start=False, stop=True).then_inc(hist_done, 1)

            pe.wait_ge(seg_step, 2)
            nc.tensor.matmul(before_ps, below[0:NT, 0:NT], upto[:, P - 1:P], start=True, stop=True).then_inc(before_made, 1)
            pe.wait_ge(seg_step, 4)
            nc.tensor.transpose(seg_ps[:, 0:NT], end_row[:, :], ident[0:NT, 0:NT])
            nc.tensor.transpose(seg_ps[:, NT:], count[:, :], ident[0:NT, 0:NT]).then_inc(seg_moved, 1)

            pe.wait_ge(copied1, NCH1)
            pe.wait_ge(bias_ready, 2)

            def turn_agg1(q):
                pe.wait_ge(agg1_ready, q + 1)
                if q > 0:
                    pe.wait_ge(agg1_t_ready, q)
                for j, t in enumerate(GROUPS[q]):
                    last = nc.tensor.transpose(bank[2][0:FE, j * P:(j + 1) * P], agg1[:, t, :], ident[:, :])
                last.then_inc(agg1_turned, 1)

            def gin(q):
                pe.wait_ge(agg1_t_ready, q + 1)
                if q > 0:
                    pe.wait_ge(x1_ready, q)
                for j in range(len(GROUPS[q])):
                    last = nc.tensor.matmul(bank[3][:, j * F:(j + 1) * F], agg1_t[:, q % 2, j, :], wgin[:, :],
                                            start=True, stop=True)
                last.then_inc(gin_done, 1)

            for q in range(AHEAD):
                turn_agg1(q)
                gin(q)
            for q in range(NG):
                turn_h(q, 1)
                if q + AHEAD < NG:
                    turn_agg1(q + AHEAD)
                pe.wait_ge(ht_ready, NG + q + 1)
                if q > 0:
                    pe.wait_ge(b_ready, q)
                times(bank[6], q, w1[:, 1, :], b_made)
                if q + AHEAD < NG:
                    gin(q + AHEAD)
                if q > 0:
                    pe.wait_ge(a_ready, q)
                times(bank[5], q, w1[:, 0, :], a_made)

            pe.wait_ge(x1_ready, NG)
            pe.wait_ge(ht_ready, 2 * NG)

            def front2(i, k):
                c, k4 = RING2 * i + k, k % RING
                peeled = isinstance(i, int) and i == 0
                hot = k4 == 0 and not (peeled and k == 0)
                pe.wait_ge(seeds_loaded[k4], 32 * i + 16 * (k // RING) + 16)
                if not peeled or k >= 2:
                    pe.wait_ge(filled2, c - 1)
                for j in range(TPC):
                    last = nc.tensor.transpose(bank[k % 2][:, j::TPC], seeds[:, k4, j, :], ident[:, :])
                last.then_inc(seeds_t, 1)
                pe.wait_ge(edges_loaded[k4], 32 * i + 16 * (k // RING) + 16)
                if not peeled or k >= 2:
                    pe.wait_ge(pre_ready, c - 1)
                nc.tensor.matmul(bank[2 + k % 2], w1[:, 2, :], edges[:, k4, :], start=True, stop=False)
                each, more = gathers2(k)
                pe.wait_ge(got2[k], 16 * (each * (i + 1) + more))
                for j in range(TPG if hot else TPC):
                    last = nc.tensor.matmul(bank[2 + k % 2][:, j * P:(j + 1) * P], rows[:, k, j, :], ident[:, :],
                                            start=False, stop=(j == TPC - 1))
                if hot:
                    pe.wait_ge(row2_split, 2 * i + k // RING)
                    for part in range(NSPLIT):
                        last = nc.tensor.matmul(bank[2 + k % 2][:, TPG * P:], row_parts2[:, part, :], ident_bf[:, :],
                                                start=False, stop=(part == NSPLIT - 1))
                last.then_inc(summed, 1)

            def back_2(i, k):
                c = RING2 * i + k
                peeled = isinstance(i, int) and i == 0
                pe.wait_ge(scanned2, c + 1)
                if not peeled or k >= 2:
                    pe.wait_ge(copied2, c - 1)
                for j in range(TPC):
                    last = nc.tensor.transpose(bank[4 + k % 2][:, j * P:(j + 1) * P], scan[:, k % 2, j::TPC],
                                               ident[:, :])
                last.then_inc(back2, 1)

            def spread2_src(n):
                pe.wait_ge(staged2, n + 1)
                if not (isinstance(n, int) and n == 0):
                    pe.wait_ge(hot2_ready, RING * n)
                nc.tensor.transpose(src_ps2, src_m2[:, 0:1].to_broadcast([P, P]), ident_h[:, :]).then_inc(spread2, 1)

            def quarter2(i, k):
                c = RING2 * i + k
                pe.wait_ge(hot2_ready, c + 1)
                if k % RING == 0 and not (isinstance(i, int) and c == 0):
                    pe.wait_ge(row2_split, 2 * i + k // RING)
                for t in QUARTERS[k % RING]:
                    last = nc.tensor.matmul(row_ps2, hot_src2[:, t, :], b_parts[:, t, 0:NSPLIT * F],
                                            start=(t == 0), stop=(t == NT - 1))
                last.then_inc(quarter_done, 1)

            def work2(i, k, last=False):
                front2(i, k)
                if k % RING == 2 and not last:
                    spread2_src(2 * i + k // RING + 1)
                if not (last and k >= RING):
                    quarter2(i, k)
                if not (isinstance(i, int) and i == 0 and k == 0):
                    back_2(i if k else i - 1, (k - 1) % RING2)

            pe.wait_ge(b_ready, NG)
            spread2_src(0)
            pe.wait_ge(b_parts_ready, NG)
            for k in range(RING2):
                work2(0, k)
            with pe.Fori(1, NCH // RING2 - 1) as i:
                for k in range(RING2):
                    work2(i, k)
            for k in range(RING2):
                work2(NCH // RING2 - 1, k, last=True)
            back_2(NCH // RING2 - 1, RING2 - 1)

            pe.wait_ge(pre_ready, NCH)
            pe.wait_ge(copied2, NCH)
            for q in range(NG):
                for j, t in enumerate(GROUPS[q]):
                    nc.tensor.matmul(bank[q][:, j * F:(j + 1) * F], ht[:, t, :], w2[:, 0, :], start=(j == 0), stop=False)

            def turn_agg2(q):
                pe.wait_ge(agg2_ready, q + 1)
                if q > 0:
                    pe.wait_ge(agg2_t_ready, q)
                for j, t in enumerate(GROUPS[q]):
                    last = nc.tensor.transpose(bank[7][:, j * P:(j + 1) * P], agg2[:, t, 0:F], ident[:, :])
                last.then_inc(agg2_turned, 1)

            for q, g in enumerate(GROUPS):
                turn_agg2(q)
                pe.wait_ge(agg2_t_ready, q + 1)
                for j in range(len(g)):
                    last = nc.tensor.matmul(bank[q][:, j * F:(j + 1) * F], agg2_t[:, q % 2, j, :], w2[:, 1, :],
                                            start=False, stop=(j == len(g) - 1))
                last.then_inc(out_prod, 1)


def kernel(x, src, dst, edge_attr_128, L0_gnn_W_fs, L0_gnn_b_fs, L0_gnn_W_gn, L0_gnn_b_gn, L0_gnn_W_gin,
           L0_gnn_b_gin, L1_gnn_u, L1_gnn_W1, L1_gnn_b1, L1_gnn_W2, L1_gnn_b2):
    import numpy as np
    import concourse.bacc as bacc
    from concourse.bass_utils import run_bass_kernel_spmd

    x, src, dst, e = (np.asarray(a) for a in (x, src, dst, edge_attr_128))
    src_pad = np.concatenate([src, np.zeros(EPAD - N_EDGES, src.dtype)])
    e_pad = np.concatenate([e, np.zeros((EPAD - N_EDGES, F), e.dtype)])
    arrays = {
        "x": np.concatenate([x, np.zeros((NPAD - N_NODES, F), x.dtype)]),
        "src1": src_pad.reshape(2, NCH1, TPC, P).transpose(1, 3, 2, 0)[:, :, :TPG, :].reshape(NCH1, P, 2 * TPG),
        "src_hot1": src_pad.reshape(2, NCH1, TPC, P)[:, :, TPG, :].transpose(2, 1, 0).reshape(P, 2 * NCH1),
        "src2": src_pad.reshape(NCH, TPC, P).transpose(0, 2, 1),
        "src_hot2": src_pad.reshape(NCH, TPC, P)[RING::RING, TPG, :].T,
        "dst": np.concatenate([np.full(1, -1, dst.dtype), dst, np.full(EPAD - N_EDGES, DST_PAD, dst.dtype)])[None, :],
        "edge_t": e_pad.reshape(NCH, CH, F).transpose(0, 2, 1),
        "w_fs": L0_gnn_W_fs, "b_fs": L0_gnn_b_fs, "w_gn": L0_gnn_W_gn, "b_gn": L0_gnn_b_gn,
        "w_gin": L0_gnn_W_gin, "b_gin": L0_gnn_b_gin, "u": L1_gnn_u, "w1_t": np.asarray(L1_gnn_W1).T,
        "b1": L1_gnn_b1, "w2_t": np.asarray(L1_gnn_W2).T, "b2": L1_gnn_b2,
    }
    arrays = {"in_" + name: np.ascontiguousarray(a) for name, a in arrays.items()}
    nc = bacc.Bacc("TRN2", target_bir_lowering=False, num_devices=1)
    ins = [nc.dram_tensor(name, a.shape, mybir.dt.from_np(a.dtype), kind="ExternalInput").ap()
           for name, a in arrays.items()]
    out = nc.dram_tensor("out", (N_NODES, F), mybir.dt.float32, kind="ExternalOutput").ap()
    gnn_program(nc, *ins, out)
    r = run_bass_kernel_spmd(nc, [arrays], core_ids=[0])
    return r.results[0]["out"]
```
